# Optimizing a Trainium2 kernel written in Bass

```python
import numpy as np
import jax
import jax.numpy as jnp

def _softmax(x, axis=-1):
    return jax.nn.softmax(x, axis=axis)

def _gelu(x):
    return jax.nn.gelu(x, approximate=True)

def _silu(x):
    return jax.nn.silu(x)

def _sigmoid(x):
    return jax.nn.sigmoid(x)

def _layernorm(x, axis=-1, eps=1e-05):
    m = jnp.mean(x, axis=axis, keepdims=True)
    v = jnp.var(x, axis=axis, keepdims=True)
    return (x - m) / jnp.sqrt(v + eps)

def _scatter_add(tgt, idx, src, axis=0):
    return tgt.at[idx].add(src)

def _segment_sum(src, seg, n):
    return jax.ops.segment_sum(src, seg, n)
kernel_name = 'mk_sandwich_d1_jaxref_r4_7fc7d1'

def setup_inputs(seed: int=0):
    np.random.seed(seed)
    _w = jnp.asarray

    def _L0_attn_setup():
        import jax, jax.numpy as jnp
        import numpy as np
        B, S, D = (2, 512, 256)
        H = 16
        HD = D // H
        SCALE = HD ** (-0.5)
        key = jax.random.key(seed)
        ks = jax.random.split(key, 9)
        init = lambda k, shape: jax.random.normal(k, shape, dtype=jnp.float32) * (1.0 / np.sqrt(shape[-1]))
        return {'x': jax.random.normal(ks[0], (B, S, D), dtype=jnp.float32), 'wq': init(ks[1], (D, D)), 'bq': jnp.zeros((D,), jnp.float32), 'wk': init(ks[2], (D, D)), 'bk': jnp.zeros((D,), jnp.float32), 'wv': init(ks[3], (D, D)), 'bv': jnp.zeros((D,), jnp.float32), 'wo': init(ks[4], (D, D)), 'bo': jnp.zeros((D,), jnp.float32)}
    _L0_attn_in = _L0_attn_setup()

    def _L0_ffn_setup():
        import jax, jax.numpy as jnp
        import numpy as np
        TOP_K = 2
        key = jax.random.key(seed)
        ks = jax.random.split(key, 6)
        B, S, D, E = (8, 1024, 256, 8)
        s = 1.0 / np.sqrt(D)
        return {'x': jax.random.normal(ks[0], (B, S, D), dtype=jnp.float32), 'Wr': jax.random.normal(ks[1], (D, E), dtype=jnp.float32) * s, 'br': jnp.zeros((E,), dtype=jnp.float32), 'W1': jax.random.normal(ks[2], (E, D, D), dtype=jnp.float32) * s, 'b1': jnp.zeros((E, D), dtype=jnp.float32), 'W2': jax.random.normal(ks[3], (E, D, D), dtype=jnp.float32) * s, 'b2': jnp.zeros((E, D), dtype=jnp.float32)}
    _L0_ffn_in = _L0_ffn_setup()
    _d = {'L0_attn_x': _L0_attn_in['x'], 'L0_attn_wq': _L0_attn_in['wq'], 'L0_attn_bq': _L0_attn_in['bq'], 'L0_attn_wk': _L0_attn_in['wk'], 'L0_attn_bk': _L0_attn_in['bk'], 'L0_attn_wv': _L0_attn_in['wv'], 'L0_attn_bv': _L0_attn_in['bv'], 'L0_attn_wo': _L0_attn_in['wo'], 'L0_attn_bo': _L0_attn_in['bo'], 'L0_ffn_Wr': _L0_ffn_in['Wr'], 'L0_ffn_br': _L0_ffn_in['br'], 'L0_ffn_W1': _L0_ffn_in['W1'], 'L0_ffn_b1': _L0_ffn_in['b1'], 'L0_ffn_W2': _L0_ffn_in['W2'], 'L0_ffn_b2': _L0_ffn_in['b2']}
    _x0 = _d['L0_attn_x']
    _d['L0_attn_x'] = jax.random.normal(jax.random.fold_in(jax.random.key(seed), 1), (4, 2048, 256), dtype=_x0.dtype)
    del _x0
    return _d

def reference(L0_attn_x, L0_attn_wq, L0_attn_bq, L0_attn_wk, L0_attn_bk, L0_attn_wv, L0_attn_bv, L0_attn_wo, L0_attn_bo, L0_ffn_Wr, L0_ffn_br, L0_ffn_W1, L0_ffn_b1, L0_ffn_W2, L0_ffn_b2):

    def _L0_attn_ref(x, wq, bq, wk, bk, wv, bv, wo, bo):
        import jax, jax.numpy as jnp
        import numpy as np
        B, S, D = (2, 512, 256)
        H = 16
        HD = D // H
        SCALE = HD ** (-0.5)
        b, s, d = x.shape
        q = (x @ wq + bq).reshape(b, s, H, HD).transpose(0, 2, 1, 3)
        k = (x @ wk + bk).reshape(b, s, H, HD).transpose(0, 2, 1, 3)
        v = (x @ wv + bv).reshape(b, s, H, HD).transpose(0, 2, 1, 3)
        scores = jnp.einsum('bhqd,bhkd->bhqk', q, k) * SCALE
        causal = jnp.tril(jnp.ones((s, s), dtype=bool))
        scores = jnp.where(causal, scores, -jnp.inf)
        weights = jax.nn.softmax(scores, axis=-1)
        out = jnp.einsum('bhqk,bhkd->bhqd', weights, v)
        out = out.transpose(0, 2, 1, 3).reshape(b, s, d)
        return out @ wo + bo

    def _L0_ffn_ref(x, Wr, br, W1, b1, W2, b2):
        import jax, jax.numpy as jnp
        import numpy as np
        TOP_K = 2
        k = TOP_K
        scores0 = x[:, 0, :] @ Wr + br
        _, idx = jax.lax.top_k(scores0, k)
        W1g, b1g = (W1[idx], b1[idx])
        W2g, b2g = (W2[idx], b2[idx])
        h = jnp.einsum('bsd,bkde->bkse', x, W1g) + b1g[:, :, None, :]
        h = jax.nn.gelu(h, approximate=False)
        o = jnp.einsum('bkse,bkef->bksf', h, W2g) + b2g[:, :, None, :]
        return jnp.sum(o, axis=1) / k
    x = L0_attn_x
    x = x + _layernorm(_L0_attn_ref(_layernorm(x, axis=-1), L0_attn_wq, L0_attn_bq, L0_attn_wk, L0_attn_bk, L0_attn_wv, L0_attn_bv, L0_attn_wo, L0_attn_bo), axis=-1)
    x = x + _layernorm(_L0_ffn_ref(_layernorm(x, axis=-1), L0_ffn_Wr, L0_ffn_br, L0_ffn_W1, L0_ffn_b1, L0_ffn_W2, L0_ffn_b2), axis=-1)
    return x

_drawn_inputs = setup_inputs


def setup_inputs(seed=0):
    import zlib

    import numpy as np

    out = dict(_drawn_inputs(seed))
    spreads = {'L0_attn_bq': (0.0, 0.1),
     'L0_attn_bk': (0.0, 0.1),
     'L0_attn_bv': (0.0, 0.1),
     'L0_attn_bo': (0.0, 0.1),
     'L0_ffn_br': (0.0, 0.1),
     'L0_ffn_b1': (0.0, 0.1),
     'L0_ffn_b2': (0.0, 0.1)}
    factors = {}
    for name, (base, spread) in spreads.items():
        noise = np.random.default_rng([zlib.crc32(name.encode()), seed]).standard_normal(out[name].shape)
        drawn = base * np.exp(spread * noise) if base else spread * noise
        out[name] = jnp.asarray(drawn.astype(out[name].dtype))
    for name, factor in factors.items():
        out[name] = (out[name] * factor).astype(out[name].dtype)
    return out
```

```python
from contextlib import ExitStack

import concourse.bass as bass
from concourse import mybir

F32 = mybir.dt.float32
BF16 = mybir.dt.bfloat16
I32 = mybir.dt.int32
ALU = mybir.AluOpType
ACT = mybir.ActivationFunctionType
AX = mybir.AxisListType

P = 128
B, S, D = 4, 2048, 256
H, HD = 16, 16
E = 8
KD = D // P
CH = 512
TT = CH // P
NC = S // CH
NT = S // P
HG = 4
NG = H // HG
VW = 32
EPS = 1e-5
SCALE = float(HD) ** -0.5
NEG = -1e30

SLOTS = [(0, 0), (0, 1), (1, 0), (0, 2), (1, 1), (2, 0)]
KR = HD * len(SLOTS)


class Chain:

    def __init__(self, eng, sem, base):
        self.eng, self.sem, self.base, self.n = eng, sem, base, 0

    def mark(self, ins):
        self.n += 1
        ins.then_inc(self.sem, 1)

    def wait(self):
        self.eng.wait_ge(self.sem, self.base + self.n)


LN_MARKS = 4


class LayerNorm:

    def __init__(self, nc, sb, name):
        self.nc = nc
        self.stats = sb(name + "_stats", [P, TT, 6], F32)
        self.tmp = sb(name + "_tmp", [P, 4, TT], F32)
        self.mean = sb(name + "_mean", [P, TT], F32)
        self.var = sb(name + "_var", [P, TT], F32)
        self.std = sb(name + "_std", [P, TT], F32)
        self.rstd = sb(name + "_rstd", [P, TT], F32)

    def variance(self, chain, src, var_done):
        v, st, tmp = self.nc.vector, self.stats, self.tmp
        for t in range(TT):
            last = v.bn_stats(st[:, t, :], src[:, t])
        chain.mark(last)
        chain.wait()
        v.tensor_tensor(tmp[:, 0, :], st[:, :, 1], st[:, :, 4], ALU.subtract)
        v.tensor_tensor(tmp[:, 1, :], st[:, :, 2], st[:, :, 5], ALU.add)
        chain.mark(v.tensor_tensor(tmp[:, 2, :], st[:, :, 1], st[:, :, 4], ALU.add))
        chain.wait()
        v.scalar_tensor_tensor(out=tmp[:, 3, :], in0=tmp[:, 0, :], scalar=float(D // 4), in1=tmp[:, 0, :],
                               op0=ALU.mult, op1=ALU.mult)
        chain.mark(v.tensor_scalar(self.mean[:, :], tmp[:, 2, :], 0.5, None, ALU.mult))
        chain.wait()
        v.tensor_tensor(self.var[:, :], tmp[:, 3, :], tmp[:, 1, :], ALU.add).then_inc(var_done, 1)

    def root(self, eps, std_done):
        self.nc.scalar.activation(self.std[:, :], self.var[:, :], ACT.Sqrt, bias=eps[:, 0:1],
                                  scale=1.0 / D).then_inc(std_done, 1)

    def normalise(self, chain, src, dst):
        v = self.nc.vector
        chain.mark(v.reciprocal(self.rstd[:, :], self.std[:, :]))
        chain.wait()
        for t in range(TT):
            last = v.tensor_scalar(dst[:, t], src[:, t], self.mean[:, t:t + 1], self.rstd[:, t:t + 1],
                                   ALU.subtract, ALU.mult)
        return last


def make_identity(nc, pool, ident, const, count):
    nc.gpsimd.memset(ident[:, :], 0.0).then_inc(const, 1)
    pool.wait_ge(const, count + 1)
    nc.gpsimd.affine_select(out=ident[:, :], in_=ident[:, :], compare_op=ALU.not_equal, fill=1.0,
                            base=0, pattern=[[-1, P]], channel_multiplier=1).then_inc(const, 1)


def stage_a(nc, ins, qk_scr, v_scr):
    with ExitStack() as ctx:
        def sb(name, shape, dt):
            return ctx.enter_context(nc.sbuf_tensor(name, shape, dt))

        def pb(name, shape, dt):
            return ctx.enter_context(nc.psum_tensor(name, shape, dt))

        def sem(name):
            return ctx.enter_context(nc.semaphore(name))

        ident = sb("a_ident", [P, P], F32)
        w = sb("a_w", [P, 3, KD, D], F32)
        bqk = sb("a_bqk", [P, 2, KD], F32)
        bqs = sb("a_bqs", [P, KD], F32)
        bvb = sb("a_bv", [P, D], F32)
        epsc = sb("a_eps", [P, 1], F32)
        x_sb = sb("a_x", [P, 2, TT, D], F32)
        xn = sb("a_xn", [P, 2, TT, D], F32)
        xT = sb("a_xT", [P, 2, KD, CH], F32)
        full = sb("a_full", [P, 2 * KD, CH], F32)
        rest = sb("a_rest", [P, 2 * KD, CH], F32)
        parts = sb("a_parts", [P, 2, 2 * KD, 3, CH], BF16)
        v_sb = sb("a_v", [P, 2, TT, H * VW], F32)
        ln = LayerNorm(nc, sb, "a_ln")
        psT = pb("a_psT", [P, KD, CH], F32)
        psQK = pb("a_psQK", [P, 2 * KD, CH], F32)
        psV = pb("a_psV", [P, TT, D], F32)

        w_ld = sem("a_w_ld")
        x_ld = [sem(f"a_x_ld{p}") for p in range(2)]
        const = sem("a_const")
        chain_s = sem("a_chain")
        var_done = sem("a_var_done")
        std_done = sem("a_std_done")
        xn_done = sem("a_xn_done")
        turned = sem("a_turned")
        xT_done = sem("a_xT_done")
        qk_done = sem("a_qk_done")
        full_s = sem("a_full_done")
        hi_done = sem("a_hi_done")
        rest_done = sem("a_rest_done")
        mid_done = sem("a_mid_done")
        v_done = sem("a_v_done")
        chunk_done = sem("a_chunk_done")
        stored = [sem(f"a_stored{p}") for p in range(2)]
        STORES = 2 * KD + NG

        x_t = ins["x"].rearrange("b (c t p) d -> (b c) p t d", p=P, t=TT)
        block = ctx.enter_context(nc.Block())

        def batches(eng, body):
            with eng.Fori(0, B - 1) as b:
                body(b, False)
            body(B - 1, True)

        @block.sync
        def _(sp):
            sp.dma_start(x_sb[:, 0], x_t[0]).then_inc(x_ld[0], 16)
            for i, name in enumerate(("wq", "wk", "wv")):
                sp.dma_start(w[:, i], ins[name].rearrange("(k p) n -> p k n", p=P)).then_inc(w_ld, 16)
            with nc.allow_non_contiguous_dma(reason="512 words of bias"):
                for i, name in enumerate(("bq", "bk")):
                    sp.dma_start(bqk[:, i], ins[name].rearrange("(k p) -> p k", p=P)).then_inc(w_ld, 16)
            sp.dma_start(bvb[:, :], ins["bv"].partition_broadcast(P)).then_inc(w_ld, 16)
            sp.dma_start(x_sb[:, 1], x_t[1]).then_inc(x_ld[1], 16)

            def body(b, last):
                for c in range(NC):
                    n = b * NC + c
                    p = c % 2
                    if not (last and c >= NC - 2):
                        sp.wait_ge(xn_done, n + 1)
                        sp.dma_start(x_sb[:, p], x_t[bass.ds(n + 2, 1)].rearrange("a p t d -> p (a t) d")
                                     ).then_inc(x_ld[p], 16)
                    sp.wait_ge(chunk_done, n + 1)
                    for t in range(2):
                        for m in range(KD):
                            sp.dma_start(qk_scr[t, :, bass.ds(b * D + m * P, P), c * CH:(c + 1) * CH]
                                         .rearrange("s p n -> p s n"),
                                         parts[:, p, t * KD + m]).then_inc(stored[p], 16)
                    for g in range(NG):
                        sp.dma_start(v_scr[bass.ds(b * NG + g, 1), c * CH:(c + 1) * CH, :]
                                     .rearrange("a (t p) n -> p (a t) n", p=P),
                                     v_sb[:, p, :, g * HG * VW:(g + 1) * HG * VW]).then_inc(stored[p], 16)

            batches(sp, body)
            for p in range(2):
                sp.wait_ge(stored[p], 16 + 16 * STORES * B * NC // 2)

        @block.gpsimd
        def _(pool):
            make_identity(nc, pool, ident, const, 0)
            nc.gpsimd.memset(v_sb[:, :, :, :], 0.0).then_inc(const, 1)
            nc.gpsimd.memset(epsc[:, :], EPS).then_inc(const, 1)
            pool.wait_ge(const, 4)
            nc.gpsimd.memset(v_sb[:, :, :, :].rearrange("p b t (h e) -> p (b t h) e", e=VW)[:, :, HD:HD + 1],
                             1.0).then_inc(const, 1)

        CONST = 5

        @block.vector
        def _(v):
            def normalise(b, c):
                n = b * NC + c
                p = c % 2
                chain = Chain(v, chain_s, n * LN_MARKS)
                v.wait_ge(x_ld[p], (b * 2 + c // 2 + 1) * 16)
                ln.variance(chain, x_sb[:, p], var_done)
                v.wait_ge(std_done, n + 1)
                ln.normalise(chain, x_sb[:, p], xn[:, p]).then_inc(xn_done, 1)

            def body(b, last):
                for c in range(NC):
                    n = b * NC + c
                    p = c % 2
                    if not (last and c == NC - 1):
                        if c + 1 < NC:
                            normalise(b, c + 1)
                        else:
                            normalise(b + 1, 0)
                    else:
                        v.wait_ge(chunk_done, n)
                    v.wait_ge(hi_done, n + 1)
                    nc.vector.tensor_tensor(rest[:, :, :], full[:, :, :], parts[:, p, :, 0],
                                            ALU.subtract).then_inc(rest_done, 1)
                    v.wait_ge(mid_done, n + 1)
                    nc.vector.tensor_tensor(parts[:, p, :, 2], rest[:, :, :], parts[:, p, :, 1], ALU.subtract)
                    v.wait_ge(v_done, n + 1)
                    for t in range(0, TT, 2):
                        ins_ = nc.vector.tensor_tensor(
                            v_sb[:, p, t:t + 2].rearrange("p t (h e) -> p t h e", e=VW)[:, :, :, 0:HD],
                            psV[:, t:t + 2].rearrange("p t (h e) -> p t h e", e=HD),
                            bvb[:, :].rearrange("p (h e) -> p h e", e=HD).unsqueeze(1).to_broadcast([P, 2, H, HD]),
                            ALU.add)
                    ins_.then_inc(chunk_done, 1)

            v.wait_ge(const, CONST)
            v.wait_ge(w_ld, 6 * 16)
            nc.vector.tensor_scalar(bqs[:, :], bqk[:, 0], SCALE, None, ALU.mult).then_inc(const, 1)
            normalise(0, 0)
            batches(v, body)

        @block.scalar
        def _(act):
            def root(b, c):
                act.wait_ge(var_done, b * NC + c + 1)
                ln.root(epsc, std_done)

            def copy_xT(b, c):
                act.wait_ge(turned, b * NC + c + 1)
                nc.scalar.copy(xT[:, c % 2], psT[:, :, :]).then_inc(xT_done, 1)

            def body(b, last):
                for c in range(NC):
                    n = b * NC + c
                    p = c % 2
                    after = None if last and c == NC - 1 else (b, c + 1) if c + 1 < NC else (b + 1, 0)
                    if after:
                        root(*after)
                    for i in range(2 * KD):
                        act.wait_ge(qk_done, n * 2 * KD + i + 1)
                        t, m = divmod(i, KD)
                        nc.scalar.activation(full[:, i], psQK[:, i], ACT.Identity,
                                             bias=bqs[:, m:m + 1] if t == 0 else bqk[:, 1, m:m + 1],
                                             scale=SCALE if t == 0 else 1.0).then_inc(full_s, 1)
                    if after:
                        copy_xT(*after)
                    act.wait_ge(stored[p], 16 + (b * 2 + c // 2) * 16 * STORES)
                    act.wait_ge(full_s, (n + 1) * 2 * KD)
                    nc.scalar.copy(parts[:, p, :, 0], full[:, :, :]).then_inc(hi_done, 1)
                    act.wait_ge(rest_done, n + 1)
                    nc.scalar.copy(parts[:, p, :, 1], rest[:, :, :]).then_inc(mid_done, 1)

            act.wait_ge(const, CONST + 1)
            for p in range(2):
                act.sem_inc(stored[p], 16)
            root(0, 0)
            copy_xT(0, 0)
            batches(act, body)

        @block.tensor
        def _(pe):
            def turn(b, c):
                pe.wait_ge(xn_done, b * NC + c + 1)
                for k in range(KD):
                    for t in range(TT):
                        ins_ = nc.tensor.transpose(psT[:, k, t * P:(t + 1) * P], xn[:, c % 2, t, k * P:(k + 1) * P],
                                                   ident[:, :])
                ins_.then_inc(turned, 1)

            def body(b, last):
                for c in range(NC):
                    n = b * NC + c
                    p = c % 2
                    pe.wait_ge(xT_done, n + 1)
                    for i in range(2 * KD):
                        t, m = divmod(i, KD)
                        for k in range(KD):
                            ins_ = nc.tensor.matmul(psQK[:, i], w[:, t, k, m * P:(m + 1) * P], xT[:, p, k],
                                                    start=(k == 0), stop=(k == KD - 1))
                        ins_.then_inc(qk_done, 1)
                    if c + 1 < NC:
                        turn(b, c + 1)
                    elif not last:
                        turn(b + 1, 0)
                    else:
                        pe.wait_ge(chunk_done, n)
                    for t in range(TT):
                        for k in range(KD):
                            ins_ = nc.tensor.matmul(psV[:, t], xT[:, p, k, t * P:(t + 1) * P], w[:, 2, k],
                                                    start=(k == 0), stop=(k == KD - 1))
                    ins_.then_inc(v_done, 1)

            pe.wait_ge(const, CONST)
            pe.wait_ge(w_ld, 6 * 16)
            turn(0, 0)
            batches(pe, body)



GK = sum(TT * (c + 1) for c in range(NC))
BK = 2 * GK
KEY_STEPS = [(g, c, kt) for g in range(2) for c in range(NC) for kt in range(TT * (c + 1))]
PIECES = [(g, c, h, qt, pc) for g in range(2) for c in range(NC) for h in range(HG) for qt in range(TT)
          for pc in range(c + 1)]
PER_STEP = len(PIECES) // BK
LEAD = 20
PV_LAG = 2
BANKS = 3
PBUF = 4
NPAIR = B * NG // 2


def piece_jobs(j):
    jobs = []
    at = PER_STEP * j
    for i in range(at, at + PER_STEP):
        g, c, h, qt, pc = PIECES[i % len(PIECES)]
        jobs.append(("piece", g, c, h, qt, pc, i + 1 == len(PIECES) or PIECES[(i + 1) % len(PIECES)][:2] != (g, c)))
    ended = PIECES[(at - 1) % len(PIECES)][:2]
    if at and ended != PIECES[at % len(PIECES)][:2]:
        jobs.append(("turn_max", *ended))
    return jobs


def out_jobs(j):
    s = j - PV_LAG - 2
    if j == BK + 2:
        s = BK - 1
    if 0 <= s < BK and (s + 1 == BK or KEY_STEPS[s + 1][:2] != KEY_STEPS[s][:2]) and (s != BK - 1 or j == BK + 2):
        return [("turn_out", *KEY_STEPS[s][:2])]
    return []


def pair_jobs(last):
    steps = []
    for j in range(BK + 3):
        jobs = []
        m = {BK: BK - 2, BK + 1: BK - 1, BK - 2: None, BK - 1: None}.get(j, j)
        if m is not None and m < BK and not (last and m + LEAD > BK):
            jobs += [x for x in piece_jobs(m + LEAD) if not (last and m + LEAD == BK and x[0] == "piece")]
        steps.append(jobs + out_jobs(j))
    return steps


LEAD_JOBS = [piece_jobs(j) for j in range(LEAD)]
BODY_JOBS = pair_jobs(False)
LAST_JOBS = pair_jobs(True)
N_LEAD = sum(map(len, LEAD_JOBS))
N_BODY = sum(map(len, BODY_JOBS))
assert N_BODY % BANKS == 0 and BK % PBUF == 0


def stage_b(nc, qk_scr, v_scr, ctx_all):
    with ExitStack() as ctx:
        def sb(name, shape, dt):
            return ctx.enter_context(nc.sbuf_tensor(name, shape, dt))

        def pb(name, shape, dt):
            return ctx.enter_context(nc.psum_tensor(name, shape, dt))

        def sem(name):
            return ctx.enter_context(nc.semaphore(name))

        ident = sb("b_ident", [P, P], F32)
        identb = sb("b_identb", [P, P], BF16)
        above = sb("b_above", [P, P], BF16)
        qT = sb("b_qT", [P, 2, HG, S], BF16)
        kT = sb("b_kT", [P, 2, HG, S], BF16)
        vS = sb("b_v", [P, 2, NT, HG * VW], F32)
        prob = sb("b_prob", [P, PBUF, HG, CH], F32)
        pmax = sb("b_pmax", [P, 2, HG * TT, NC], F32)
        nmax = sb("b_nmax", [P, 2, HG * TT], F32)
        nmT = sb("b_nmT", [HG * TT, 2, P], BF16)
        outT = sb("b_outT", [P, 2, CH], F32)
        rsum = sb("b_rsum", [P, 2, TT, HG], F32)
        psS = pb("b_psS", [P, HG, CH], F32)
        ring = pb("b_ring", [P, BANKS, CH], F32)
        psO = pb("b_psO", [P, CH], F32)

        const = sem("b_const")
        loaded = [sem(f"b_loaded{p}") for p in range(2)]
        nm_ld = [[sem(f"b_nm{p}{c}") for c in range(NC)] for p in range(2)]
        ring_full = sem("b_ring_full")
        ring_free = sem("b_ring_free")
        nm_done = sem("b_nm_done")
        scored = sem("b_scored")
        exp_done = sem("b_exp_done")
        stood = sem("b_stood")
        masked = sem("b_masked")
        pv_done = sem("b_pv_done")
        out_copied = sem("b_out_copied")
        out_turned = sem("b_out_turned")
        LOADS = 2 * len(SLOTS) + 2
        CHUNKS = 2 * NC

        block = ctx.enter_context(nc.Block())

        def pairs(eng, body):
            with eng.Fori(0, NPAIR - 1) as it:
                body(it, BODY_JOBS, False)
            body(NPAIR - 1, LAST_JOBS, True)

        def chunk_index(it, g, c):
            return it * CHUNKS + g * NC + c

        @block.sync
        def _(sp):
            def load(it, g):
                at = it * 2 + g
                for t, buf in enumerate((qT, kT)):
                    for s, slot in enumerate(SLOTS):
                        sp.dma_start(buf[s * HD:(s + 1) * HD, g],
                                     qk_scr[t, slot[t], bass.ds(at * HG * HD, HG * HD), :]
                                     .rearrange("(h d) n -> d h n", d=HD)).then_inc(loaded[g], 16)
                for t in range(0, NT, NT // 2):
                    sp.dma_start(vS[:, g, t:t + NT // 2], v_scr[bass.ds(at, 1), t * P:(t + NT // 2) * P]
                                 .rearrange("a (t p) n -> p (a t) n", p=P)).then_inc(loaded[g], 16)

            def place_max(g, c, r):
                sp.wait_ge(ring_free, r + 1)
                for h in range(HG):
                    sp.dma_start(qT[KR:KR + 1, g % 2, h, c * CH:(c + 1) * CH].rearrange("o (q n) -> o q n", n=P),
                                 nmT[h * TT:(h + 1) * TT, c % 2, :]).then_inc(nm_ld[g % 2][c], 16)

            def body(it, steps, last):
                r = it * N_BODY + N_LEAD
                for j, jobs in enumerate(steps):
                    for job in jobs:
                        if job[0] == "turn_max":
                            place_max(job[1], job[2], r)
                        r = r + 1
                    if j == GK + PV_LAG + 1 and not last:
                        sp.wait_ge(pv_done, it * BK + GK + PBUF)
                        load(it + 1, 0)
                if not last:
                    sp.wait_ge(pv_done, it * BK + BK + PBUF)
                    load(it + 1, 1)

            load(0, 0)
            load(0, 1)
            r = 0
            for jobs in LEAD_JOBS:
                for job in jobs:
                    if job[0] == "turn_max":
                        place_max(job[1], job[2], r)
                    r += 1
            pairs(sp, body)

        @block.gpsimd
        def _(pool):
            make_identity(nc, pool, ident, const, 0)
            pool.wait_ge(const, 2)
            nc.gpsimd.memset(kT[KR:KR + 1, :, :, :], 1.0).then_inc(const, 1)
            pool.wait_ge(const, 3)
            nc.gpsimd.memset(above[:, :], 0.0).then_inc(const, 1)
            pool.wait_ge(const, 4)
            nc.gpsimd.tensor_copy(identb[:, :], ident[:, :]).then_inc(const, 1)
            nc.gpsimd.affine_select(out=above[:, :], in_=above[:, :], compare_op=ALU.is_ge, fill=NEG,
                                    base=0, pattern=[[-1, P]], channel_multiplier=1).then_inc(const, 1)

            def body(it, steps, last):
                for j, (g, c, kt) in enumerate(KEY_STEPS):
                    i = kt - TT * c
                    if i >= 0:
                        pool.wait_ge(exp_done, it * 2 * BK + 2 * (j + 1) + 2)
                        pool.sem_inc(stood, 1)
                        tile = prob[:, j % PBUF, :, i * P:(i + 1) * P]
                        nc.gpsimd.affine_select(out=tile, in_=tile, compare_op=ALU.is_ge, fill=0.0, base=0,
                                                pattern=[[0, HG], [1, P]], channel_multiplier=-1
                                                ).then_inc(masked, 1)

            pairs(pool, body)

        CONST = 6

        def ends_chunk(s):
            return s + 1 == BK or KEY_STEPS[s + 1][:2] != KEY_STEPS[s][:2]

        @block.vector
        def _(v):
            def do(job, r, bank, it):
                if job[0] == "piece":
                    _, g, c, h, qt, pc, ends = job
                    w = min(CH, (TT * c + qt + 1) * P - pc * CH)
                    v.wait_ge(ring_full, r + 1)
                    nc.vector.tensor_reduce(pmax[:, c % 2, h * TT + qt, pc:pc + 1], ring[:, bank, 0:w], AX.X,
                                            ALU.max).then_inc(ring_free, 1)
                    if ends:
                        v.wait_ge(ring_free, r + 1)
                        nc.vector.tensor_reduce(nmax[:, c % 2], pmax[:, c % 2, :, 0:c + 1], AX.X, ALU.max,
                                                negate=True).then_inc(nm_done, 1)
                elif job[0] == "turn_max":
                    _, g, c = job
                    v.wait_ge(ring_full, r + 1)
                    if it is not None:
                        bg, bc = (g, c - 2) if c >= 2 else (1 - g, c + 2)
                        v.wait_ge(nm_ld[bg][bc], (it + 1) * 16 * HG)
                    nc.vector.tensor_copy(nmT[:, c % 2], ring[0:HG * TT, bank, 0:P]).then_inc(ring_free, 1)
                else:
                    _, g, c = job
                    v.wait_ge(ring_full, r + 1)
                    o = ring[:, bank, :].rearrange("p (t h e) -> p t h e", t=TT, h=HG)
                    nc.vector.reciprocal(rsum[:, c % 2], o[:, :, :, HD]).then_inc(out_turned, 1)
                    v.wait_ge(out_turned, chunk_index(it, g, c) + 1 + 2)
                    at = (it * 2 + g) * NT + c * TT
                    nc.vector.tensor_tensor(
                        ctx_all[:, bass.ds(at, TT), :].rearrange("p t (h e) -> p t h e", e=HD),
                        o[:, :, :, 0:HD], rsum[:, c % 2].unsqueeze(3).to_broadcast([P, TT, HG, HD]),
                        ALU.mult).then_inc(ring_free, 1)

            def body(it, steps, last):
                i = N_LEAD
                for jobs in steps:
                    for job in jobs:
                        do(job, it * N_BODY + i, i % BANKS, it)
                        i += 1

            v.sem_inc(out_turned, 2)
            r = 0
            for jobs in LEAD_JOBS:
                for job in jobs:
                    do(job, r, r % BANKS, None)
                    r += 1
            pairs(v, body)

        @block.scalar
        def _(act):
            def body(it, steps, last):
                for j in range(BK + PV_LAG):
                    if j < BK:
                        g, c, kt = KEY_STEPS[j]
                        off = max(0, kt - TT * c) * P
                        act.wait_ge(pv_done, it * BK + j + 1 - PBUF + PBUF)
                        for s in range(2):
                            act.wait_ge(scored, it * 2 * BK + 2 * j + s + 1)
                            nc.scalar.activation(prob[:, j % PBUF, 2 * s:2 * s + 2, off:CH],
                                                 psS[:, 2 * s:2 * s + 2, off:CH], ACT.Exp).then_inc(exp_done, 1)
                    s = j - PV_LAG
                    if s >= 0 and ends_chunk(s):
                        g, c, _ = KEY_STEPS[s]
                        x = chunk_index(it, g, c)
                        act.wait_ge(pv_done, it * BK + s + 1 + PBUF)
                        act.wait_ge(out_turned, x - 1 + 2)
                        nc.scalar.copy(outT[:, c % 2], psO[:, :]).then_inc(out_copied, 1)

            act.sem_inc(exp_done, 2)
            act.sem_inc(out_copied, 1)
            pairs(act, body)

        @block.tensor
        def _(pe):
            def do(job, r, bank):
                if not (isinstance(r, int) and r < BANKS):
                    pe.wait_ge(ring_free, r + 1 - BANKS)
                if job[0] == "piece":
                    _, g, c, h, qt, pc, ends = job
                    t = TT * c + qt
                    w = min(CH, (t + 1) * P - pc * CH)
                    diagonal = pc == c
                    ins_ = nc.tensor.matmul(ring[:, bank, 0:w], qT[0:KR, g, h, t * P:(t + 1) * P],
                                            kT[0:KR, g, h, pc * CH:pc * CH + w], start=True, stop=not diagonal)
                    if diagonal:
                        ins_ = nc.tensor.matmul(ring[:, bank, w - P:w], identb[:, :], above[:, :],
                                                start=False, stop=True)
                    ins_.then_inc(ring_full, 1)
                elif job[0] == "turn_max":
                    _, g, c = job
                    nc.tensor.transpose(ring[0:HG * TT, bank, 0:P], nmax[:, c % 2], ident[:, :]
                                        ).then_inc(ring_full, 1)
                else:
                    _, g, c = job
                    for t in range(TT):
                        ins_ = nc.tensor.transpose(ring[:, bank, t * P:(t + 1) * P],
                                                   outT[:, c % 2, t * P:(t + 1) * P], ident[:, :])
                    ins_.then_inc(ring_full, 1)

            def body(it, steps, last):
                i = N_LEAD
                maxed = it * CHUNKS + 2
                for j, jobs in enumerate(steps):
                    half = (len(jobs) + 1) // 2
                    for s in range(2):
                        if j < BK:
                            g, c, kt = KEY_STEPS[j]
                            off = max(0, kt - TT * c) * P
                            if kt == 0 and s == 0:
                                pe.wait_ge(nm_ld[g][c], (it + 1) * 16 * HG)
                            pe.wait_ge(exp_done, it * 2 * BK + 2 * j + s - 1 + 2)
                            for h in (2 * s, 2 * s + 1):
                                ins_ = nc.tensor.matmul(psS[:, h, off:CH], kT[0:KR + 1, g, h, kt * P:(kt + 1) * P],
                                                        qT[0:KR + 1, g, h, c * CH + off:(c + 1) * CH],
                                                        start=True, stop=True)
                            ins_.then_inc(scored, 1)
                        for job in (jobs[:half], jobs[half:])[s]:
                            if job[0] == "piece" and job[2:6] == (0, 0, 0, 0):
                                nxt = 1 if j > GK else 0
                                pe.wait_ge(loaded[job[1]], (it + 1 + nxt) * 16 * LOADS)
                            if job[0] == "turn_max":
                                maxed = maxed + 1
                                pe.wait_ge(nm_done, maxed)
                            if job[0] == "turn_out":
                                pe.wait_ge(out_copied, chunk_index(it, job[1], job[2]) + 1 + 1)
                            do(job, it * N_BODY + i, i % BANKS)
                            i += 1
                    jj = j - PV_LAG
                    if 0 <= jj < BK:
                        g, c, kt = KEY_STEPS[jj]
                        off = max(0, kt - TT * c) * P
                        if kt >= TT * c:
                            diag = sum(1 for (_, c2, k2) in KEY_STEPS[:jj + 1] if k2 >= TT * c2)
                            pe.wait_ge(masked, it * (2 * NT) + diag)
                        else:
                            pe.wait_ge(exp_done, it * 2 * BK + 2 * (jj + 1) + 2)
                        if kt == 0:
                            pe.wait_ge(out_copied, chunk_index(it, g, c) + 1)
                        for h in range(HG):
                            ins_ = nc.tensor.matmul(psO[h * VW:(h + 1) * VW, off:CH],
                                                    vS[:, g, kt, h * VW:(h + 1) * VW],
                                                    prob[:, jj % PBUF, h, off:CH],
                                                    start=(kt == 0), stop=(kt == TT * (c + 1) - 1))
                        ins_.then_inc(pv_done, 1)

            pe.wait_ge(const, CONST)
            pe.sem_inc(pv_done, PBUF)
            r = 0
            for j, jobs in enumerate(LEAD_JOBS):
                for job in jobs:
                    if r == 0:
                        pe.wait_ge(loaded[0], 16 * LOADS)
                    if job[0] == "turn_max":
                        pe.wait_ge(nm_done, job[2] + 1)
                    do(job, r, r % BANKS)
                    r += 1
            pairs(pe, body)


def stage_c(nc, ins, ctx_all, out):
    with ExitStack() as ctx:
        def sb(name, shape, dt):
            return ctx.enter_context(nc.sbuf_tensor(name, shape, dt))

        def pb(name, shape, dt):
            return ctx.enter_context(nc.psum_tensor(name, shape, dt))

        def sem(name):
            return ctx.enter_context(nc.semaphore(name))

        ident = sb("c_ident", [P, P], F32)
        epsc = sb("c_eps", [P, 1], F32)
        wo = sb("c_wo", [P, KD, D], F32)
        bob = sb("c_bo", [P, D], F32)
        wr = sb("c_wr", [P, KD, E], F32)
        br = sb("c_br", [1, E], F32)
        x_sb = sb("c_x", [P, 2, TT, D], F32)
        cc = sb("c_cc", [P, 2, TT, D], F32)
        ccT = sb("c_ccT", [P, KD, CH], F32)
        attn = sb("c_attn", [P, TT, D], F32)
        x1 = sb("c_x1", [P, 2, TT, D], F32)
        x1_kept = sb("c_x1_kept", [P, NC, TT, D], F32)
        y = sb("c_y", [P, TT, D], F32)
        yT = sb("c_yT", [P, KD, NC, CH], F32)
        w1e = sb("c_w1e", [P, 2, KD, D], F32)
        w2e = sb("c_w2e", [P, 2, KD, D], F32)
        b1e = sb("c_b1e", [P, 2, KD], F32)
        b2e = sb("c_b2e", [P, 2, D], F32)
        b2half = sb("c_b2half", [P, D], F32)
        b2mean = sb("c_b2mean", [P, D], F32)
        hT = sb("c_hT", [P, 2, KD, CH], F32)
        ffn = sb("c_ffn", [P, TT, D], F32)
        out_sb = sb("c_out", [P, 2, TT, D], F32)
        place = sb("c_place", [1, E], F32)
        rt = sb("c_rt", [1, 6, E], F32)
        best = sb("c_best", [1, 4], F32)
        chosen = sb("c_chosen", [1, 2], I32)
        ln_a = LayerNorm(nc, sb, "c_ln_a")
        ln_x = LayerNorm(nc, sb, "c_ln_x")
        ln_f = LayerNorm(nc, sb, "c_ln_f")
        psT = pb("c_psT", [P, KD, CH], F32)
        psA = pb("c_psA", [P, TT, D], F32)
        psH = pb("c_psH", [P, 2, CH], F32)
        psO = pb("c_psO", [P, TT, D], F32)

        const = sem("c_const")
        w_ld = sem("c_w_ld")
        in_ld = [sem(f"c_in_ld{p}") for p in range(2)]
        ctx_turned = sem("c_ctx_turned")
        ccT_done = sem("c_ccT_done")
        a_done = sem("c_a_done")
        a_read = sem("c_a_read")
        chain_a, chain_x, chain_f = sem("c_chain_a"), sem("c_chain_x"), sem("c_chain_f")
        var_a, var_x, var_f = sem("c_var_a"), sem("c_var_x"), sem("c_var_f")
        std_a, std_x, std_f = sem("c_std_a"), sem("c_std_x"), sem("c_std_f")
        norm_a = sem("c_norm_a")
        x1_done = sem("c_x1_done")
        kept = [sem(f"c_kept{p}") for p in range(2)]
        y_done = sem("c_y_done")
        y_turned = sem("c_y_turned")
        yT_done = sem("c_yT_done")
        logits = sem("c_logits")
        chain_r = sem("c_chain_r")
        idx_done = sem("c_idx_done")
        stood = sem("c_stood")
        exp_ld = sem("c_exp_ld")
        h_done = sem("c_h_done")
        gelu_done = sem("c_gelu_done")
        o_done = sem("c_o_done")
        o_read = sem("c_o_read")
        chain_b = sem("c_chain_b")
        norm_f = sem("c_norm_f")
        out_done = sem("c_out_done")
        stored = [sem(f"c_stored{p}") for p in range(2)]
        EXP_LOADS = 8
        IN_LOADS = 1 + NG

        x_t = ins["x"].rearrange("b (c t p) d -> (b c) p t d", p=P, t=TT)
        out_t = out.rearrange("b (c t p) d -> (b c) p t d", p=P, t=TT)
        block = ctx.enter_context(nc.Block())


        @block.sync
        def _(sp):
            def load(b, c):
                n = b * NC + c
                p = c % 2
                sp.dma_start(x_sb[:, p], x_t[bass.ds(n, 1)].rearrange("a p t d -> p (a t) d")).then_inc(in_ld[p], 16)
                for g in range(NG):
                    sp.dma_start(cc[:, p, :, g * HG * HD:(g + 1) * HG * HD],
                                 ctx_all[:, bass.ds((b * NG + g) * NT + c * TT, TT), :]).then_inc(in_ld[p], 16)

            def load_after(b, c):
                sp.wait_ge(x1_done, b * NC + c + 1)
                if c + 2 < NC:
                    load(b, c + 2)
                else:
                    load(b + 1, c - 2)

            def keep(b, c):
                sp.wait_ge(x1_done, b * NC + c + 1)
                sp.dma_start(x1_kept[:, c], x1[:, c % 2]).then_inc(kept[c % 2], 16)

            def load_experts(b):
                sp.wait_ge(idx_done, b + 1)
                sp.sem_inc(stood, 1)
                for i in range(2):
                    e = sp.value_load(chosen[0:1, i:i + 1], min_val=0, max_val=E - 1)
                    sp.dma_start(w1e[:, i], ins["w1"][bass.ds(e, 1)].rearrange("a (k p) n -> p (a k) n", p=P)
                                 ).then_inc(exp_ld, 16)
                    sp.dma_start(w2e[:, i], ins["w2"][bass.ds(e, 1)].rearrange("a (k p) n -> p (a k) n", p=P)
                                 ).then_inc(exp_ld, 16)
                    with nc.allow_non_contiguous_dma(reason="256 words of bias"):
                        sp.dma_start(b1e[:, i], ins["b1"][bass.ds(e, 1)].rearrange("a (k p) -> p (a k)", p=P)
                                     ).then_inc(exp_ld, 16)
                    sp.dma_start(b2e[:, i], ins["b2"][bass.ds(e, 1)].rearrange("a d -> (a d)").partition_broadcast(P)
                                 ).then_inc(exp_ld, 16)

            def store(b, c):
                n = b * NC + c
                sp.wait_ge(out_done, n + 1)
                sp.dma_start(out_t[bass.ds(n, 1)].rearrange("a p t d -> p (a t) d"), out_sb[:, c % 2]
                             ).then_inc(stored[c % 2], 16)

            load(0, 0)
            sp.dma_start(wo[:, :], ins["wo"].rearrange("(k p) n -> p k n", p=P)).then_inc(w_ld, 16)
            sp.dma_start(wr[:, :], ins["wr"].rearrange("(k p) n -> p k n", p=P)).then_inc(w_ld, 16)
            sp.dma_start(bob[:, :], ins["bo"].partition_broadcast(P)).then_inc(w_ld, 16)
            sp.dma_start(br[:, :], ins["br"].unsqueeze(0)).then_inc(w_ld, 16)
            load(0, 1)
            for c in range(NC):
                load_after(0, c)
                keep(0, c)
                if c == 0:
                    load_experts(0)
            with sp.Fori(0, B - 2) as b:
                for c in range(NC):
                    load_after(b + 1, c)
                    store(b, c)
                    keep(b + 1, c)
                sp.wait_ge(o_done, (b + 1) * NC)
                load_experts(b + 1)
            for c in range(NC):
                if c < NC - 2:
                    load_after(B - 1, c)
                store(B - 2, c)
                keep(B - 1, c)
            sp.wait_ge(o_done, (B - 1) * NC)
            load_experts(B - 1)
            for c in range(NC):
                store(B - 1, c)
            for p in range(2):
                sp.wait_ge(stored[p], 16 + 16 * B * NC // 2)

        @block.gpsimd
        def _(pool):
            make_identity(nc, pool, ident, const, 0)
            pool.wait_ge(const, 2)
            nc.gpsimd.memset(epsc[:, :], EPS).then_inc(const, 1)
            pool.wait_ge(const, 3)
            for e in range(E):
                nc.gpsimd.memset(place[:, e:e + 1], float(e - E)).then_inc(const, 1)
                pool.wait_ge(const, 4 + e)

        CONST = 3 + E

        @block.vector
        def _(v):
            def attn_end(b, c):
                n = b * NC + c
                p = c % 2
                v.wait_ge(in_ld[p], (b * 2 + c // 2 + 1) * 16 * IN_LOADS)
                v.wait_ge(a_done, n + 1)
                nc.vector.tensor_tensor(attn[:, :, :], psA[:, :, :],
                                        bob[:, :].unsqueeze(1).to_broadcast([P, TT, D]), ALU.add
                                        ).then_inc(a_read, 1)
                v.wait_ge(a_read, n + 1)
                chain = Chain(v, chain_a, n * LN_MARKS)
                ln_a.variance(chain, attn, var_a)
                v.wait_ge(std_a, n + 1)
                ln_a.normalise(chain, attn, attn).then_inc(norm_a, 1)
                v.wait_ge(norm_a, n + 1)
                k = b * 2 + c // 2
                if not isinstance(b, int) or k > 0:
                    v.wait_ge(kept[p], k * 16)
                nc.vector.tensor_tensor(x1[:, p], x_sb[:, p], attn[:, :, :], ALU.add).then_inc(x1_done, 1)
                v.wait_ge(x1_done, n + 1)
                chain = Chain(v, chain_x, n * LN_MARKS)
                ln_x.variance(chain, x1[:, p], var_x)
                v.wait_ge(std_x, n + 1)
                ln_x.normalise(chain, x1[:, p], y).then_inc(y_done, 1)

            def route(b):
                chain = Chain(v, chain_r, b * 9)
                v.wait_ge(logits, b + 1)
                chain.mark(nc.vector.tensor_tensor(rt[:, 0], psA[0:1, 0, 0:E], br[:, :], ALU.add))
                for i in range(2):
                    score, equal, where = rt[:, 3 * i], rt[:, 3 * i + 1], rt[:, 3 * i + 2]
                    top, at = best[:, 2 * i:2 * i + 1], best[:, 2 * i + 1:2 * i + 2]
                    chain.wait()
                    chain.mark(nc.vector.tensor_reduce(top, score, AX.X, ALU.max))
                    chain.wait()
                    chain.mark(nc.vector.scalar_tensor_tensor(out=where, in0=score, scalar=top, in1=place[:, :],
                                                              op0=ALU.is_equal, op1=ALU.mult))
                    chain.wait()
                    chain.mark(nc.vector.tensor_reduce(at, where, AX.X, ALU.min))
                    chain.wait()
                    if i == 0:
                        chain.mark(nc.vector.tensor_scalar(equal, place[:, :], at, -3.0e38, ALU.is_equal, ALU.mult))
                        chain.wait()
                        chain.mark(nc.vector.tensor_tensor(rt[:, 3], score, equal, ALU.add))
                nc.vector.tensor_scalar(chosen[:, :], best[:, :].rearrange("o (i two) -> o i two", two=2)[:, :, 1],
                                        float(E), None, ALU.add).then_inc(idx_done, 1)

            def experts_end(b, c):
                n = b * NC + c
                p = c % 2
                if c == 0:
                    v.wait_ge(exp_ld, (b + 1) * 16 * EXP_LOADS)
                    nc.vector.tensor_scalar(b2half[:, :], b2e[:, 0], 0.5, None, ALU.mult).then_inc(chain_b, 1)
                    v.wait_ge(chain_b, b * 2 + 1)
                    nc.vector.scalar_tensor_tensor(out=b2mean[:, :], in0=b2e[:, 1], scalar=0.5, in1=b2half[:, :],
                                                   op0=ALU.mult, op1=ALU.add).then_inc(chain_b, 1)
                    v.wait_ge(chain_b, b * 2 + 2)
                if isinstance(b, int):
                    v.wait_ge(out_done, n)
                v.wait_ge(o_done, n + 1)
                nc.vector.scalar_tensor_tensor(out=ffn[:, :, :], in0=psO[:, :, :], scalar=0.5,
                                               in1=b2mean[:, :].unsqueeze(1).to_broadcast([P, TT, D]),
                                               op0=ALU.mult, op1=ALU.add).then_inc(o_read, 1)
                v.wait_ge(o_read, n + 1 + 1)
                chain = Chain(v, chain_f, n * LN_MARKS)
                ln_f.variance(chain, ffn, var_f)
                v.wait_ge(std_f, n + 1)
                ln_f.normalise(chain, ffn, ffn).then_inc(norm_f, 1)
                v.wait_ge(norm_f, n + 1)
                v.wait_ge(stored[p], 16 + (b * 2 + c // 2) * 16)
                v.wait_ge(kept[p], (b * 2 + c // 2 + 1) * 16)
                nc.vector.tensor_tensor(out_sb[:, p], x1_kept[:, c], ffn[:, :, :], ALU.add).then_inc(out_done, 1)

            v.wait_ge(const, CONST)
            v.wait_ge(w_ld, 4 * 16)
            v.sem_inc(o_read, 1)
            for p in range(2):
                v.sem_inc(stored[p], 16)
            for c in range(NC):
                attn_end(0, c)
                if c == 0:
                    route(0)
            with v.Fori(0, B - 1) as b:
                for c in range(NC):
                    attn_end(b + 1, c)
                    experts_end(b, c)
                    if c == 0:
                        route(b + 1)
            for c in range(NC):
                experts_end(B - 1, c)

        @block.scalar
        def _(act):
            def copy_ctx(b, c):
                act.wait_ge(ctx_turned, b * NC + c + 1)
                nc.scalar.copy(ccT[:, :, :], psT[:, :, :]).then_inc(ccT_done, 1)

            def attn_end(b, c):
                n = b * NC + c
                act.wait_ge(var_a, n + 1)
                ln_a.root(epsc, std_a)
                act.wait_ge(var_x, n + 1)
                ln_x.root(epsc, std_x)
                act.wait_ge(y_turned, n + 1)
                nc.scalar.copy(yT[:, :, c], psT[:, :, :]).then_inc(yT_done, 1)

            def gelu(b, c):
                n = b * NC + c
                if c == 0:
                    act.wait_ge(exp_ld, (b + 1) * 16 * EXP_LOADS)
                for i in range(2 * KD):
                    e, m = divmod(i, KD)
                    act.wait_ge(h_done, n * 2 * KD + i + 1)
                    nc.scalar.activation(hT[:, e, m], psH[:, i % 2], ACT.Gelu, bias=b1e[:, e, m:m + 1]
                                         ).then_inc(gelu_done, 1)

            def experts_end(b, c):
                act.wait_ge(var_f, b * NC + c + 1)
                ln_f.root(epsc, std_f)

            act.wait_ge(const, CONST)
            act.sem_inc(gelu_done, 2)
            for c in range(NC):
                copy_ctx(0, c)
                attn_end(0, c)
            with act.Fori(0, B - 1) as b:
                for c in range(NC):
                    copy_ctx(b + 1, c)
                    gelu(b, c)
                    attn_end(b + 1, c)
                    experts_end(b, c)
            for c in range(NC):
                gelu(B - 1, c)
                experts_end(B - 1, c)

        @block.tensor
        def _(pe):
            def turn_ctx(b, c):
                n = b * NC + c
                p = c % 2
                pe.wait_ge(in_ld[p], (b * 2 + c // 2 + 1) * 16 * IN_LOADS)
                for k in range(KD):
                    for t in range(TT):
                        ins_ = nc.tensor.transpose(psT[:, k, t * P:(t + 1) * P], cc[:, p, t, k * P:(k + 1) * P],
                                                   ident[:, :])
                ins_.then_inc(ctx_turned, 1)

            def project(b, c):
                n = b * NC + c
                pe.wait_ge(ccT_done, n + 1)
                if c == 1:
                    pe.wait_ge(idx_done, b + 1)
                for t in range(TT):
                    for k in range(KD):
                        ins_ = nc.tensor.matmul(psA[:, t], ccT[:, k, t * P:(t + 1) * P], wo[:, k],
                                                start=(k == 0), stop=(k == KD - 1))
                ins_.then_inc(a_done, 1)

            def turn_y(b, c):
                n = b * NC + c
                pe.wait_ge(y_done, n + 1)
                for k in range(KD):
                    for t in range(TT):
                        ins_ = nc.tensor.transpose(psT[:, k, t * P:(t + 1) * P], y[:, t, k * P:(k + 1) * P],
                                                   ident[:, :])
                ins_.then_inc(y_turned, 1)
                pe.wait_ge(yT_done, n + 1)
                if c == 0:
                    for k in range(KD):
                        ins_ = nc.tensor.matmul(psA[0:1, 0, 0:E], yT[:, k, 0, 0:1], wr[:, k],
                                                start=(k == 0), stop=(k == KD - 1))
                    ins_.then_inc(logits, 1)

            def hidden(b, c):
                n = b * NC + c
                if c == 0:
                    pe.wait_ge(exp_ld, (b + 1) * 16 * EXP_LOADS)
                pe.wait_ge(yT_done, n + 1)
                for i in range(2 * KD):
                    e, m = divmod(i, KD)
                    pe.wait_ge(gelu_done, n * 2 * KD + i - 1 + 2)
                    for k in range(KD):
                        ins_ = nc.tensor.matmul(psH[:, i % 2], w1e[:, e, k, m * P:(m + 1) * P], yT[:, k, c],
                                                start=(k == 0), stop=(k == KD - 1))
                    ins_.then_inc(h_done, 1)

            def outer(b, c):
                n = b * NC + c
                pe.wait_ge(gelu_done, (n + 1) * 2 * KD + 2)
                pe.wait_ge(o_read, n + 1)
                for t in range(TT):
                    for i in range(2 * KD):
                        e, m = divmod(i, KD)
                        ins_ = nc.tensor.matmul(psO[:, t], hT[:, e, m, t * P:(t + 1) * P], w2e[:, e, m],
                                                start=(i == 0), stop=(i == 2 * KD - 1))
                ins_.then_inc(o_done, 1)

            pe.wait_ge(const, CONST)
            pe.wait_ge(w_ld, 4 * 16)
            for c in range(NC):
                turn_ctx(0, c)
                project(0, c)
                turn_y(0, c)
            with pe.Fori(0, B - 1) as b:
                for c in range(NC):
                    turn_ctx(b + 1, c)
                    hidden(b, c)
                    project(b + 1, c)
                    outer(b, c)
                    turn_y(b + 1, c)
            for c in range(NC):
                hidden(B - 1, c)
                outer(B - 1, c)


def program(nc, ins, out):
    qk_scr = nc.dram_tensor("qk_parts", (2, 3, B * D, S), BF16, kind="Internal").ap()
    v_scr = nc.dram_tensor("v_ones", (B * NG, S, HG * VW), F32, kind="Internal").ap()
    stage_a(nc, ins, qk_scr, v_scr)
    with nc.sbuf_tensor("ctx_all", [P, B * NG * NT, HG * HD], F32) as ctx_all:
        stage_b(nc, qk_scr, v_scr, ctx_all)
        stage_c(nc, ins, ctx_all, out)


_NAMES = {"x": "L0_attn_x", "wq": "L0_attn_wq", "bq": "L0_attn_bq", "wk": "L0_attn_wk", "bk": "L0_attn_bk",
          "wv": "L0_attn_wv", "bv": "L0_attn_bv", "wo": "L0_attn_wo", "bo": "L0_attn_bo", "wr": "L0_ffn_Wr",
          "br": "L0_ffn_br", "w1": "L0_ffn_W1", "b1": "L0_ffn_b1", "w2": "L0_ffn_W2", "b2": "L0_ffn_b2"}


def kernel(**inputs):
    import numpy as _np
    import concourse.bacc as _bacc
    from concourse import mybir as _mybir
    from concourse.bass_utils import run_bass_kernel_spmd as _run

    nc = _bacc.Bacc("TRN2", target_bir_lowering=False, num_devices=1)
    arrays, aps = {}, {}
    for short, name in _NAMES.items():
        a = _np.ascontiguousarray(inputs[name])
        arrays[f"in_{name}"] = a
        aps[short] = nc.dram_tensor(f"in_{name}", a.shape, _mybir.dt.from_np(a.dtype), kind="ExternalInput").ap()
    out = nc.dram_tensor("out_0", (B, S, D), F32, kind="ExternalOutput").ap()
    program(nc, aps, out)
    r = _run(nc, [arrays], core_ids=[0])
    return r.results[0]["out_0"]
```

```python
from contextlib import ExitStack

import concourse.bass as bass
from concourse import mybir

F32 = mybir.dt.float32
BF16 = mybir.dt.bfloat16
I32 = mybir.dt.int32
ALU = mybir.AluOpType
ACT = mybir.ActivationFunctionType
AX = mybir.AxisListType

P = 128
B, S, D = 4, 2048, 256
H, HD = 16, 16
E = 8
KD = D // P
CH = 512
TT = CH // P
NC = S // CH
NT = S // P
HG = 4
NG = H // HG
VW = 32
EPS = 1e-5
SCALE = float(HD) ** -0.5
NEG = -1e30

SLOTS = [(0, 0), (0, 1), (1, 0), (0, 2), (1, 1), (2, 0)]
KR = HD * len(SLOTS)


class Chain:

    def __init__(self, eng, sem, base):
        self.eng, self.sem, self.base, self.n = eng, sem, base, 0

    def mark(self, ins):
        self.n += 1
        ins.then_inc(self.sem, 1)

    def wait(self):
        self.eng.wait_ge(self.sem, self.base + self.n)


LN_MARKS = 4


class LayerNorm:

    def __init__(self, nc, sb, name):
        self.nc = nc
        self.stats = sb(name + "_stats", [P, TT, 6], F32)
        self.tmp = sb(name + "_tmp", [P, 4, TT], F32)
        self.mean = sb(name + "_mean", [P, TT], F32)
        self.var = sb(name + "_var", [P, TT], F32)
        self.std = sb(name + "_std", [P, TT], F32)
        self.rstd = sb(name + "_rstd", [P, TT], F32)

    def variance(self, chain, src, var_done):
        v, st, tmp = self.nc.vector, self.stats, self.tmp
        for t in range(TT):
            last = v.bn_stats(st[:, t, :], src[:, t])
        chain.mark(last)
        chain.wait()
        v.tensor_tensor(tmp[:, 0, :], st[:, :, 1], st[:, :, 4], ALU.subtract)
        v.tensor_tensor(tmp[:, 1, :], st[:, :, 2], st[:, :, 5], ALU.add)
        chain.mark(v.tensor_tensor(tmp[:, 2, :], st[:, :, 1], st[:, :, 4], ALU.add))
        chain.wait()
        v.scalar_tensor_tensor(out=tmp[:, 3, :], in0=tmp[:, 0, :], scalar=float(D // 4), in1=tmp[:, 0, :],
                               op0=ALU.mult, op1=ALU.mult)
        chain.mark(v.tensor_scalar(self.mean[:, :], tmp[:, 2, :], 0.5, None, ALU.mult))
        chain.wait()
        v.tensor_tensor(self.var[:, :], tmp[:, 3, :], tmp[:, 1, :], ALU.add).then_inc(var_done, 1)

    def root(self, eps, std_done):
        self.nc.scalar.activation(self.std[:, :], self.var[:, :], ACT.Sqrt, bias=eps[:, 0:1],
                                  scale=1.0 / D).then_inc(std_done, 1)

    def normalise(self, chain, src, dst):
        v = self.nc.vector
        chain.mark(v.reciprocal(self.rstd[:, :], self.std[:, :]))
        chain.wait()
        for t in range(TT):
            last = v.tensor_scalar(dst[:, t], src[:, t], self.mean[:, t:t + 1], self.rstd[:, t:t + 1],
                                   ALU.subtract, ALU.mult)
        return last


class Constants:

    IDENT, EPS_SET, BUILT = 2, 3, 6 + E
    LOADS = 4

    def __init__(self, nc, ctx):
        def sb(name, shape, dt):
            return ctx.enter_context(nc.sbuf_tensor(name, shape, dt))

        self.nc = nc
        self.ident = sb("ident", [P, P], F32)
        self.identb = sb("identb", [P, P], BF16)
        self.above = sb("above", [P, P], BF16)
        self.eps = sb("eps", [P, 1], F32)
        self.place = sb("place", [1, E], F32)
        self.wo = sb("wo", [P, KD, D], F32)
        self.bo = sb("bo", [P, D], F32)
        self.wr = sb("wr", [P, KD, E], F32)
        self.br = sb("br", [1, E], F32)
        self.set = ctx.enter_context(nc.semaphore("const_set"))
        self.loaded = ctx.enter_context(nc.semaphore("const_loaded"))

    def build_first(self, pool):
        self.nc.gpsimd.memset(self.ident[:, :], 0.0).then_inc(self.set, 1)
        pool.wait_ge(self.set, 1)
        self.nc.gpsimd.affine_select(out=self.ident[:, :], in_=self.ident[:, :], compare_op=ALU.not_equal,
                                     fill=1.0, base=0, pattern=[[-1, P]], channel_multiplier=1
                                     ).then_inc(self.set, 1)
        self.nc.gpsimd.memset(self.eps[:, :], EPS).then_inc(self.set, 1)

    def build_rest(self, pool):
        self.nc.gpsimd.memset(self.above[:, :], 0.0).then_inc(self.set, 1)
        pool.wait_ge(self.set, 4)
        self.nc.gpsimd.tensor_copy(self.identb[:, :], self.ident[:, :]).then_inc(self.set, 1)
        self.nc.gpsimd.affine_select(out=self.above[:, :], in_=self.above[:, :], compare_op=ALU.is_ge, fill=NEG,
                                     base=0, pattern=[[-1, P]], channel_multiplier=1).then_inc(self.set, 1)
        for e in range(E):
            pool.wait_ge(self.set, 6 + e)
            self.nc.gpsimd.memset(self.place[:, e:e + 1], float(e - E)).then_inc(self.set, 1)

    def load(self, sp, ins):
        sp.dma_start(self.wo[:, :], ins["wo"].rearrange("(k p) n -> p k n", p=P)).then_inc(self.loaded, 16)
        sp.dma_start(self.wr[:, :], ins["wr"].rearrange("(k p) n -> p k n", p=P)).then_inc(self.loaded, 16)
        sp.dma_start(self.bo[:, :], ins["bo"].partition_broadcast(P)).then_inc(self.loaded, 16)
        sp.dma_start(self.br[:, :], ins["br"].unsqueeze(0)).then_inc(self.loaded, 16)


class Groups:

    LOADS = 2 * len(SLOTS) + 2

    def __init__(self, nc, ctx, qk_scr, v_scr):
        self.nc, self.qk_scr, self.v_scr = nc, qk_scr, v_scr
        self.qT = ctx.enter_context(nc.sbuf_tensor("g_qT", [P, 2, HG, S], BF16))
        self.kT = ctx.enter_context(nc.sbuf_tensor("g_kT", [P, 2, HG, S], BF16))
        self.vS = ctx.enter_context(nc.sbuf_tensor("g_v", [P, 2, NT, HG * VW], F32))
        self.loaded = [ctx.enter_context(nc.semaphore(f"g_loaded{p}")) for p in range(2)]

    def write_ones(self, done):
        self.nc.gpsimd.memset(self.kT[KR:KR + 1, :, :, :], 1.0).then_inc(done, 1)

    def load(self, sp, at, g):
        for t, buf in enumerate((self.qT, self.kT)):
            for s, slot in enumerate(SLOTS):
                sp.dma_start(buf[s * HD:(s + 1) * HD, g],
                             self.qk_scr[t, slot[t], bass.ds(at * HG * HD, HG * HD), :]
                             .rearrange("(h d) n -> d h n", d=HD)).then_inc(self.loaded[g], 16)
        for t in range(0, NT, NT // 2):
            sp.dma_start(self.vS[:, g, t:t + NT // 2], self.v_scr[bass.ds(at, 1), t * P:(t + NT // 2) * P]
                         .rearrange("a (t p) n -> p (a t) n", p=P)).then_inc(self.loaded[g], 16)


def stage_a(nc, ins, qk_scr, v_scr, consts, groups, shared):
    with ExitStack() as ctx:
        def sb(name, shape, dt):
            return ctx.enter_context(nc.sbuf_tensor(name, shape, dt))

        def pb(name, shape, dt):
            return ctx.enter_context(nc.psum_tensor(name, shape, dt))

        def sem(name):
            return ctx.enter_context(nc.semaphore(name))

        ident = consts.ident
        w = sb("a_w", [P, 3, KD, D], F32)
        bqk = sb("a_bqk", [P, 2, KD], F32)
        bqs = sb("a_bqs", [P, KD], F32)
        bvb = sb("a_bv", [P, D], F32)
        room = 2 * TT * D
        x_sb, xn = (shared[:, i * room:(i + 1) * room].rearrange("p (b t d) -> p b t d", b=2, t=TT) for i in range(2))
        xT = shared[:, 2 * room:3 * room].rearrange("p (b k n) -> p b k n", b=2, k=KD)
        full, rest = (shared[:, i * room:(i + 1) * room].rearrange("p (i n) -> p i n", i=2 * KD) for i in (3, 4))
        parts = sb("a_parts", [P, 2, 2 * KD, 3, CH], BF16)
        v_sb = sb("a_v", [P, 2, TT, H * VW], F32)
        ln = LayerNorm(nc, sb, "a_ln")
        psT = pb("a_psT", [P, KD, CH], F32)
        psQK = pb("a_psQK", [P, 2 * KD, CH], F32)
        psV = pb("a_psV", [P, TT, D], F32)

        w_ld = sem("a_w_ld")
        x_ld = [sem(f"a_x_ld{p}") for p in range(2)]
        v_set = sem("a_v_set")
        b_scaled = sem("a_b_scaled")
        chain_s = sem("a_chain")
        var_done = sem("a_var_done")
        std_done = sem("a_std_done")
        xn_done = sem("a_xn_done")
        turned = sem("a_turned")
        xT_done = sem("a_xT_done")
        qk_done = sem("a_qk_done")
        full_s = sem("a_full_done")
        hi_done = sem("a_hi_done")
        rest_done = sem("a_rest_done")
        mid_done = sem("a_mid_done")
        v_done = sem("a_v_done")
        chunk_done = sem("a_chunk_done")
        stored = [sem(f"a_stored{p}") for p in range(2)]
        STORES = 2 * KD + NG

        x_t = ins["x"].rearrange("b (c t p) d -> (b c) p t d", p=P, t=TT)
        block = ctx.enter_context(nc.Block())

        def batches(eng, body):
            with eng.Fori(0, B - 1) as b:
                body(b, False)
            body(B - 1, True)

        @block.sync
        def _(sp):
            sp.dma_start(x_sb[:, 0], x_t[0]).then_inc(x_ld[0], 16)
            for i, name in enumerate(("wq", "wk", "wv")):
                sp.dma_start(w[:, i], ins[name].rearrange("(k p) n -> p k n", p=P)).then_inc(w_ld, 16)
            with nc.allow_non_contiguous_dma(reason="512 words of bias"):
                for i, name in enumerate(("bq", "bk")):
                    sp.dma_start(bqk[:, i], ins[name].rearrange("(k p) -> p k", p=P)).then_inc(w_ld, 16)
            sp.dma_start(bvb[:, :], ins["bv"].partition_broadcast(P)).then_inc(w_ld, 16)
            sp.dma_start(x_sb[:, 1], x_t[1]).then_inc(x_ld[1], 16)

            def body(b, last):
                for c in range(NC):
                    n = b * NC + c
                    p = c % 2
                    if not (last and c >= NC - 3):
                        sp.wait_ge(xn_done, n + 2)
                        load_x(n + 3, 1 - p)
                    sp.wait_ge(chunk_done, n + 1 + 1)
                    for t in range(2):
                        for m in range(KD):
                            sp.dma_start(qk_scr[t, :, bass.ds(b * D + m * P, P), c * CH:(c + 1) * CH]
                                         .rearrange("s p n -> p s n"),
                                         parts[:, p, t * KD + m]).then_inc(stored[p], 16)
                    for g in range(NG):
                        sp.dma_start(v_scr[bass.ds(b * NG + g, 1), c * CH:(c + 1) * CH, :]
                                     .rearrange("a (t p) n -> p (a t) n", p=P),
                                     v_sb[:, p, :, g * HG * VW:(g + 1) * HG * VW]).then_inc(stored[p], 16)
                    if last and c == 0:
                        for q in range(2):
                            sp.wait_ge(stored[q], 16 + 16 * STORES * NC // 2)
                        groups.load(sp, 0, 0)

            def load_x(n, p):
                sp.dma_start(x_sb[:, p], x_t[bass.ds(n, 1)].rearrange("a p t d -> p (a t) d")).then_inc(x_ld[p], 16)

            sp.wait_ge(xn_done, 1)
            load_x(2, 0)
            batches(sp, body)
            for p in range(2):
                sp.wait_ge(stored[p], 16 + 16 * STORES * B * NC // 2)
            consts.load(sp, ins)

        @block.gpsimd
        def _(pool):
            consts.build_first(pool)
            nc.gpsimd.memset(v_sb[:, :, :, :], 0.0).then_inc(v_set, 1)
            pool.wait_ge(v_set, 1)
            nc.gpsimd.memset(v_sb[:, :, :, :].rearrange("p b t (h e) -> p (b t h) e", e=VW)[:, :, HD:HD + 1],
                             1.0).then_inc(v_set, 1)
            pool.wait_ge(v_set, 2)
            groups.write_ones(v_set)
            pool.wait_ge(v_set, 3)
            consts.build_rest(pool)

        @block.vector
        def _(v):
            def variance(b, c):
                chain = Chain(v, chain_s, (b * NC + c) * LN_MARKS)
                v.wait_ge(x_ld[c % 2], (b * 2 + c // 2 + 1) * 16)
                ln.variance(chain, x_sb[:, c % 2], var_done)
                return chain

            def normalise(chain, b, c):
                v.wait_ge(std_done, b * NC + c + 1)
                ln.normalise(chain, x_sb[:, c % 2], xn[:, c % 2]).then_inc(xn_done, 1)

            def body(b, last):
                for c in range(NC):
                    n = b * NC + c
                    p = c % 2
                    after = (b, c + 2) if c + 2 < NC else None if last else (b + 1, c + 2 - NC)
                    if after:
                        chain = variance(*after)
                    v.wait_ge(chunk_done, n + 1)
                    v.wait_ge(hi_done, n + 1)
                    nc.vector.tensor_tensor(rest[:, :, :], full[:, :, :], parts[:, p, :, 0],
                                            ALU.subtract).then_inc(rest_done, 1)
                    if after:
                        normalise(chain, *after)
                    v.wait_ge(mid_done, n + 1)
                    nc.vector.tensor_tensor(parts[:, p, :, 2], rest[:, :, :], parts[:, p, :, 1], ALU.subtract)
                    v.wait_ge(v_done, n + 1)
                    for t in range(0, TT, 2):
                        ins_ = nc.vector.tensor_tensor(
                            v_sb[:, p, t:t + 2].rearrange("p t (h e) -> p t h e", e=VW)[:, :, :, 0:HD],
                            psV[:, t:t + 2].rearrange("p t (h e) -> p t h e", e=HD),
                            bvb[:, :].rearrange("p (h e) -> p h e", e=HD).unsqueeze(1).to_broadcast([P, 2, H, HD]),
                            ALU.add)
                    ins_.then_inc(chunk_done, 1)

            normalise(variance(0, 0), 0, 0)
            normalise(variance(0, 1), 0, 1)
            v.wait_ge(v_set, 2)
            v.wait_ge(w_ld, 6 * 16)
            nc.vector.tensor_scalar(bqs[:, :], bqk[:, 0], SCALE, None, ALU.mult).then_inc(b_scaled, 1)
            batches(v, body)

        @block.scalar
        def _(act):
            def root(b, c):
                act.wait_ge(var_done, b * NC + c + 1)
                ln.root(consts.eps, std_done)

            def copy_xT(b, c):
                act.wait_ge(turned, b * NC + c + 1)
                nc.scalar.copy(xT[:, c % 2], psT[:, :, :]).then_inc(xT_done, 1)

            def body(b, last):
                for c in range(NC):
                    n = b * NC + c
                    p = c % 2
                    after = None if last and c == NC - 1 else (b, c + 1) if c + 1 < NC else (b + 1, 0)
                    for i in range(2 * KD):
                        act.wait_ge(qk_done, n * 2 * KD + i + 1)
                        t, m = divmod(i, KD)
                        nc.scalar.activation(full[:, i], psQK[:, i], ACT.Identity,
                                             bias=bqs[:, m:m + 1] if t == 0 else bqk[:, 1, m:m + 1],
                                             scale=SCALE if t == 0 else 1.0).then_inc(full_s, 1)
                    if after:
                        copy_xT(*after)
                    act.wait_ge(stored[p], 16 + (b * 2 + c // 2) * 16 * STORES)
                    act.wait_ge(full_s, (n + 1) * 2 * KD)
                    nc.scalar.copy(parts[:, p, :, 0], full[:, :, :]).then_inc(hi_done, 1)
                    if c + 2 < NC:
                        root(b, c + 2)
                    elif not last:
                        root(b + 1, c + 2 - NC)
                    act.wait_ge(rest_done, n + 1)
                    nc.scalar.copy(parts[:, p, :, 1], rest[:, :, :]).then_inc(mid_done, 1)

            act.wait_ge(consts.set, consts.EPS_SET)
            for p in range(2):
                act.sem_inc(stored[p], 16)
            root(0, 0)
            root(0, 1)
            copy_xT(0, 0)
            act.wait_ge(b_scaled, 1)
            batches(act, body)

        @block.tensor
        def _(pe):
            def turn(b, c):
                pe.wait_ge(xn_done, b * NC + c + 1)
                for k in range(KD):
                    for t in range(TT):
                        ins_ = nc.tensor.transpose(psT[:, k, t * P:(t + 1) * P], xn[:, c % 2, t, k * P:(k + 1) * P],
                                                   ident[:, :])
                ins_.then_inc(turned, 1)

            def body(b, last):
                for c in range(NC):
                    n = b * NC + c
                    p = c % 2
                    pe.wait_ge(xT_done, n + 1)
                    for i in range(2 * KD):
                        t, m = divmod(i, KD)
                        for k in range(KD):
                            ins_ = nc.tensor.matmul(psQK[:, i], w[:, t, k, m * P:(m + 1) * P], xT[:, p, k],
                                                    start=(k == 0), stop=(k == KD - 1))
                        ins_.then_inc(qk_done, 1)
                    if c + 1 < NC:
                        turn(b, c + 1)
                    elif not last:
                        turn(b + 1, 0)
                    pe.wait_ge(chunk_done, n + 1)
                    for t in range(TT):
                        for k in range(KD):
                            ins_ = nc.tensor.matmul(psV[:, t], xT[:, p, k, t * P:(t + 1) * P], w[:, 2, k],
                                                    start=(k == 0), stop=(k == KD - 1))
                    ins_.then_inc(v_done, 1)

            pe.wait_ge(consts.set, consts.IDENT)
            pe.wait_ge(w_ld, 6 * 16)
            pe.sem_inc(chunk_done, 1)
            turn(0, 0)
            batches(pe, body)



GK = sum(TT * (c + 1) for c in range(NC))
BK = 2 * GK
KEY_STEPS = [(g, c, kt) for g in range(2) for c in range(NC) for kt in range(TT * (c + 1))]
PIECES = [(g, c, h, qt, pc) for g in range(2) for c in range(NC) for h in range(HG) for qt in range(TT)
          for pc in range(c + 1)]
PER_STEP = len(PIECES) // BK
LEAD = 20
PV_LAG = 2
BANKS = 3
PBUF = 4
NPAIR = B * NG // 2


def piece_jobs(j):
    jobs = []
    at = PER_STEP * j
    for i in range(at, at + PER_STEP):
        g, c, h, qt, pc = PIECES[i % len(PIECES)]
        jobs.append(("piece", g, c, h, qt, pc, i + 1 == len(PIECES) or PIECES[(i + 1) % len(PIECES)][:2] != (g, c)))
    ended = PIECES[(at - 1) % len(PIECES)][:2]
    if at and ended != PIECES[at % len(PIECES)][:2]:
        jobs.append(("turn_max", *ended))
    return jobs


def out_jobs(j):
    s = j - PV_LAG - 2
    if j == BK + 2:
        s = BK - 1
    if 0 <= s < BK and (s + 1 == BK or KEY_STEPS[s + 1][:2] != KEY_STEPS[s][:2]) and (s != BK - 1 or j == BK + 2):
        return [("turn_out", *KEY_STEPS[s][:2])]
    return []


def pair_jobs(last):
    steps = []
    for j in range(BK + 3):
        jobs = []
        m = {BK: BK - 2, BK + 1: BK - 1, BK - 2: None, BK - 1: None}.get(j, j)
        if m is not None and m < BK and not (last and m + LEAD > BK):
            jobs += [x for x in piece_jobs(m + LEAD) if not (last and m + LEAD == BK and x[0] == "piece")]
        steps.append(jobs + out_jobs(j))
    return steps


LEAD_JOBS = [piece_jobs(j) for j in range(LEAD)]
BODY_JOBS = pair_jobs(False)
LAST_JOBS = pair_jobs(True)
N_LEAD = sum(map(len, LEAD_JOBS))
N_BODY = sum(map(len, BODY_JOBS))
assert N_BODY % BANKS == 0 and BK % PBUF == 0


def stage_b(nc, consts, groups, ctx_all):
    with ExitStack() as ctx:
        def sb(name, shape, dt):
            return ctx.enter_context(nc.sbuf_tensor(name, shape, dt))

        def pb(name, shape, dt):
            return ctx.enter_context(nc.psum_tensor(name, shape, dt))

        def sem(name):
            return ctx.enter_context(nc.semaphore(name))

        ident, identb, above = consts.ident, consts.identb, consts.above
        qT, kT, vS, loaded = groups.qT, groups.kT, groups.vS, groups.loaded
        prob = sb("b_prob", [P, PBUF, HG, CH], F32)
        pmax = sb("b_pmax", [P, 2, HG * TT, NC], F32)
        nmax = sb("b_nmax", [P, 2, HG * TT], F32)
        nmT = sb("b_nmT", [HG * TT, 2, P], BF16)
        outT = sb("b_outT", [P, 2, CH], F32)
        rsum = sb("b_rsum", [P, 2, TT, HG], F32)
        psS = pb("b_psS", [P, HG, CH], F32)
        ring = pb("b_ring", [P, BANKS, CH], F32)
        psO = pb("b_psO", [P, CH], F32)

        nm_ld = [[sem(f"b_nm{p}{c}") for c in range(NC)] for p in range(2)]
        ring_full = sem("b_ring_full")
        ring_free = sem("b_ring_free")
        nm_done = sem("b_nm_done")
        scored = sem("b_scored")
        exp_done = sem("b_exp_done")
        stood = sem("b_stood")
        masked = sem("b_masked")
        pv_done = sem("b_pv_done")
        out_copied = sem("b_out_copied")
        out_turned = sem("b_out_turned")
        LOADS = Groups.LOADS
        CHUNKS = 2 * NC

        block = ctx.enter_context(nc.Block())

        def pairs(eng, body):
            with eng.Fori(0, NPAIR - 1) as it:
                body(it, BODY_JOBS, False)
            body(NPAIR - 1, LAST_JOBS, True)

        def chunk_index(it, g, c):
            return it * CHUNKS + g * NC + c

        @block.sync
        def _(sp):
            def place_max(g, c, r):
                sp.wait_ge(ring_free, r + 1)
                for h in range(HG):
                    sp.dma_start(qT[KR:KR + 1, g % 2, h, c * CH:(c + 1) * CH].rearrange("o (q n) -> o q n", n=P),
                                 nmT[h * TT:(h + 1) * TT, c % 2, :]).then_inc(nm_ld[g % 2][c], 16)

            def body(it, steps, last):
                r = it * N_BODY + N_LEAD
                for j, jobs in enumerate(steps):
                    for job in jobs:
                        if job[0] == "turn_max":
                            place_max(job[1], job[2], r)
                        r = r + 1
                    if j == GK + PV_LAG + 1 and not last:
                        sp.wait_ge(pv_done, it * BK + GK + PBUF)
                        groups.load(sp, it * 2 + 2, 0)
                if not last:
                    sp.wait_ge(pv_done, it * BK + BK + PBUF)
                    groups.load(sp, it * 2 + 3, 1)

            groups.load(sp, 1, 1)
            r = 0
            for jobs in LEAD_JOBS:
                for job in jobs:
                    if job[0] == "turn_max":
                        place_max(job[1], job[2], r)
                    r += 1
            pairs(sp, body)

        @block.gpsimd
        def _(pool):
            def body(it, steps, last):
                for j, (g, c, kt) in enumerate(KEY_STEPS):
                    i = kt - TT * c
                    if i >= 0:
                        pool.wait_ge(exp_done, it * 2 * BK + 2 * (j + 1) + 2)
                        pool.sem_inc(stood, 1)
                        tile = prob[:, j % PBUF, :, i * P:(i + 1) * P]
                        nc.gpsimd.affine_select(out=tile, in_=tile, compare_op=ALU.is_ge, fill=0.0, base=0,
                                                pattern=[[0, HG], [1, P]], channel_multiplier=-1
                                                ).then_inc(masked, 1)

            pairs(pool, body)

        def ends_chunk(s):
            return s + 1 == BK or KEY_STEPS[s + 1][:2] != KEY_STEPS[s][:2]

        @block.vector
        def _(v):
            def do(job, r, bank, it):
                if job[0] == "piece":
                    _, g, c, h, qt, pc, ends = job
                    w = min(CH, (TT * c + qt + 1) * P - pc * CH)
                    v.wait_ge(ring_full, r + 1)
                    nc.vector.tensor_reduce(pmax[:, c % 2, h * TT + qt, pc:pc + 1], ring[:, bank, 0:w], AX.X,
                                            ALU.max).then_inc(ring_free, 1)
                    if ends:
                        v.wait_ge(ring_free, r + 1)
                        nc.vector.tensor_reduce(nmax[:, c % 2], pmax[:, c % 2, :, 0:c + 1], AX.X, ALU.max,
                                                negate=True).then_inc(nm_done, 1)
                elif job[0] == "turn_max":
                    _, g, c = job
                    v.wait_ge(ring_full, r + 1)
                    if it is not None:
                        bg, bc = (g, c - 2) if c >= 2 else (1 - g, c + 2)
                        v.wait_ge(nm_ld[bg][bc], (it + 1) * 16 * HG)
                    nc.vector.tensor_copy(nmT[:, c % 2], ring[0:HG * TT, bank, 0:P]).then_inc(ring_free, 1)
                else:
                    _, g, c = job
                    v.wait_ge(ring_full, r + 1)
                    o = ring[:, bank, :].rearrange("p (t h e) -> p t h e", t=TT, h=HG)
                    nc.vector.reciprocal(rsum[:, c % 2], o[:, :, :, HD]).then_inc(out_turned, 1)
                    v.wait_ge(out_turned, chunk_index(it, g, c) + 1 + 2)
                    nc.vector.tensor_tensor(
                        ctx_all[:, bass.ds(it * NT + c * TT, TT), g * HG * HD:(g + 1) * HG * HD]
                        .rearrange("p t (h e) -> p t h e", e=HD),
                        o[:, :, :, 0:HD], rsum[:, c % 2].unsqueeze(3).to_broadcast([P, TT, HG, HD]),
                        ALU.mult).then_inc(ring_free, 1)

            def body(it, steps, last):
                i = N_LEAD
                for jobs in steps:
                    for job in jobs:
                        do(job, it * N_BODY + i, i % BANKS, it)
                        i += 1

            v.sem_inc(out_turned, 2)
            r = 0
            for jobs in LEAD_JOBS:
                for job in jobs:
                    do(job, r, r % BANKS, None)
                    r += 1
            pairs(v, body)

        @block.scalar
        def _(act):
            def body(it, steps, last):
                for j in range(BK + PV_LAG):
                    if j < BK:
                        g, c, kt = KEY_STEPS[j]
                        off = max(0, kt - TT * c) * P
                        act.wait_ge(pv_done, it * BK + j + 1 - PBUF + PBUF)
                        for s in range(2):
                            act.wait_ge(scored, it * 2 * BK + 2 * j + s + 1)
                            nc.scalar.activation(prob[:, j % PBUF, 2 * s:2 * s + 2, off:CH],
                                                 psS[:, 2 * s:2 * s + 2, off:CH], ACT.Exp).then_inc(exp_done, 1)
                    s = j - PV_LAG
                    if s >= 0 and ends_chunk(s):
                        g, c, _ = KEY_STEPS[s]
                        x = chunk_index(it, g, c)
                        act.wait_ge(pv_done, it * BK + s + 1 + PBUF)
                        act.wait_ge(out_turned, x - 1 + 2)
                        nc.scalar.copy(outT[:, c % 2], psO[:, :]).then_inc(out_copied, 1)

            act.sem_inc(exp_done, 2)
            act.sem_inc(out_copied, 1)
            pairs(act, body)

        @block.tensor
        def _(pe):
            def do(job, r, bank):
                if not (isinstance(r, int) and r < BANKS):
                    pe.wait_ge(ring_free, r + 1 - BANKS)
                if job[0] == "piece":
                    _, g, c, h, qt, pc, ends = job
                    t = TT * c + qt
                    w = min(CH, (t + 1) * P - pc * CH)
                    diagonal = pc == c
                    ins_ = nc.tensor.matmul(ring[:, bank, 0:w], qT[0:KR, g, h, t * P:(t + 1) * P],
                                            kT[0:KR, g, h, pc * CH:pc * CH + w], start=True, stop=not diagonal)
                    if diagonal:
                        ins_ = nc.tensor.matmul(ring[:, bank, w - P:w], identb[:, :], above[:, :],
                                                start=False, stop=True)
                    ins_.then_inc(ring_full, 1)
                elif job[0] == "turn_max":
                    _, g, c = job
                    nc.tensor.transpose(ring[0:HG * TT, bank, 0:P], nmax[:, c % 2], ident[:, :]
                                        ).then_inc(ring_full, 1)
                else:
                    _, g, c = job
                    for t in range(TT):
                        ins_ = nc.tensor.transpose(ring[:, bank, t * P:(t + 1) * P],
                                                   outT[:, c % 2, t * P:(t + 1) * P], ident[:, :])
                    ins_.then_inc(ring_full, 1)

            def body(it, steps, last):
                i = N_LEAD
                maxed = it * CHUNKS + 2
                for j, jobs in enumerate(steps):
                    half = (len(jobs) + 1) // 2
                    for s in range(2):
                        if j < BK:
                            g, c, kt = KEY_STEPS[j]
                            off = max(0, kt - TT * c) * P
                            if kt == 0 and s == 0:
                                pe.wait_ge(nm_ld[g][c], (it + 1) * 16 * HG)
                            pe.wait_ge(exp_done, it * 2 * BK + 2 * j + s - 1 + 2)
                            for h in (2 * s, 2 * s + 1):
                                ins_ = nc.tensor.matmul(psS[:, h, off:CH], kT[0:KR + 1, g, h, kt * P:(kt + 1) * P],
                                                        qT[0:KR + 1, g, h, c * CH + off:(c + 1) * CH],
                                                        start=True, stop=True)
                            ins_.then_inc(scored, 1)
                        for job in (jobs[:half], jobs[half:])[s]:
                            if job[0] == "piece" and job[2:6] == (0, 0, 0, 0):
                                nxt = 1 if j > GK else 0
                                pe.wait_ge(loaded[job[1]], (it + 1 + nxt) * 16 * LOADS)
                            if job[0] == "turn_max":
                                maxed = maxed + 1
                                pe.wait_ge(nm_done, maxed)
                            if job[0] == "turn_out":
                                pe.wait_ge(out_copied, chunk_index(it, job[1], job[2]) + 1 + 1)
                            do(job, it * N_BODY + i, i % BANKS)
                            i += 1
                    jj = j - PV_LAG
                    if 0 <= jj < BK:
                        g, c, kt = KEY_STEPS[jj]
                        off = max(0, kt - TT * c) * P
                        if kt >= TT * c:
                            diag = sum(1 for (_, c2, k2) in KEY_STEPS[:jj + 1] if k2 >= TT * c2)
                            pe.wait_ge(masked, it * (2 * NT) + diag)
                        else:
                            pe.wait_ge(exp_done, it * 2 * BK + 2 * (jj + 1) + 2)
                        if kt == 0:
                            pe.wait_ge(out_copied, chunk_index(it, g, c) + 1)
                        for h in range(HG):
                            ins_ = nc.tensor.matmul(psO[h * VW:(h + 1) * VW, off:CH],
                                                    vS[:, g, kt, h * VW:(h + 1) * VW],
                                                    prob[:, jj % PBUF, h, off:CH],
                                                    start=(kt == 0), stop=(kt == TT * (c + 1) - 1))
                        ins_.then_inc(pv_done, 1)

            pe.wait_ge(consts.set, consts.BUILT)
            pe.sem_inc(pv_done, PBUF)
            r = 0
            for j, jobs in enumerate(LEAD_JOBS):
                for job in jobs:
                    if r == 0:
                        pe.wait_ge(loaded[0], 16 * LOADS)
                    if job[0] == "turn_max":
                        pe.wait_ge(nm_done, job[2] + 1)
                    do(job, r, r % BANKS)
                    r += 1
            pairs(pe, body)


def wait_for(eng, sem, count):
    if not (isinstance(count, int) and count <= 0):
        eng.wait_ge(sem, count)


def stage_c(nc, ins, consts, ctx_all, out):
    with ExitStack() as ctx:
        def sb(name, shape, dt):
            return ctx.enter_context(nc.sbuf_tensor(name, shape, dt))

        def pb(name, shape, dt):
            return ctx.enter_context(nc.psum_tensor(name, shape, dt))

        def sem(name):
            return ctx.enter_context(nc.semaphore(name))

        ident, wo, wr, place = consts.ident, consts.wo, consts.wr, consts.place
        x_sb = sb("c_x", [P, 2, TT, D], F32)
        cc = sb("c_cc", [P, 2, KD, TT, P], F32)
        ccT = sb("c_ccT", [P, KD, CH], F32)
        attn = sb("c_attn", [P, TT, D], F32)
        x1 = sb("c_x1", [P, NC, TT, D], F32)
        y = sb("c_y", [P, TT, D], F32)
        yT = sb("c_yT", [P, KD, NC, CH], F32)
        w1e = sb("c_w1e", [P, 2, KD, D], F32)
        w2e = sb("c_w2e", [P, 2, KD, D], F32)
        b1e = sb("c_b1e", [P, 2, KD], F32)
        b2e = sb("c_b2e", [P, 2, D], F32)
        b2half = sb("c_b2half", [P, D], F32)
        b2mean = sb("c_b2mean", [P, D], F32)
        hT = sb("c_hT", [P, 2, KD, CH], F32)
        ffn = sb("c_ffn", [P, TT, D], F32)
        out_sb = sb("c_out", [P, 2, TT, D], F32)
        rt = sb("c_rt", [1, 6, E], F32)
        best = sb("c_best", [1, 4], F32)
        chosen = sb("c_chosen", [1, 2], I32)
        ln_a = LayerNorm(nc, sb, "c_ln_a")
        ln_x = LayerNorm(nc, sb, "c_ln_x")
        ln_f = LayerNorm(nc, sb, "c_ln_f")
        psT = pb("c_psT", [P, KD, CH], F32)
        psA = pb("c_psA", [P, TT, D], F32)
        psH = pb("c_psH", [P, 2, CH], F32)
        psO = pb("c_psO", [P, TT, D], F32)

        x_ld = [sem(f"c_x_ld{p}") for p in range(2)]
        cc_ld = [sem(f"c_cc_ld{p}") for p in range(2)]
        ctx_turned = sem("c_ctx_turned")
        ccT_done = sem("c_ccT_done")
        a_done = sem("c_a_done")
        a_read = sem("c_a_read")
        chain_a, chain_x, chain_f = sem("c_chain_a"), sem("c_chain_x"), sem("c_chain_f")
        var_a, var_x, var_f = sem("c_var_a"), sem("c_var_x"), sem("c_var_f")
        std_a, std_x, std_f = sem("c_std_a"), sem("c_std_x"), sem("c_std_f")
        norm_a = sem("c_norm_a")
        x1_done = sem("c_x1_done")
        y_done = sem("c_y_done")
        y_turned = sem("c_y_turned")
        yT_done = sem("c_yT_done")
        logits = sem("c_logits")
        chain_r = sem("c_chain_r")
        idx_done = sem("c_idx_done")
        stood = sem("c_stood")
        w1_ld = sem("c_w1_ld")
        w2_ld = sem("c_w2_ld")
        h_done = sem("c_h_done")
        gelu_done = sem("c_gelu_done")
        o_done = sem("c_o_done")
        o_read = sem("c_o_read")
        chain_b = sem("c_chain_b")
        norm_f = sem("c_norm_f")
        out_done = sem("c_out_done")
        stored = [sem(f"c_stored{p}") for p in range(2)]
        W_LOADS = 4

        x_t = ins["x"].rearrange("b (c t p) d -> (b c) p t d", p=P, t=TT)
        out_t = out.rearrange("b (c t p) d -> (b c) p t d", p=P, t=TT)
        block = ctx.enter_context(nc.Block())

        def ahead(b, c, k):
            b, c = b + (c + k) // NC, (c + k) % NC
            n = b * NC + c
            return None if isinstance(n, int) and not 0 <= n < B * NC else (b, c, n)

        def steps(eng, step):
            for c in range(NC):
                step(-1, c)
            with eng.Fori(0, B - 1) as b:
                for c in range(NC):
                    step(b, c)
            for c in range(NC):
                step(B - 1, c)

        @block.sync
        def _(sp):
            def load_x(n, p):
                sp.dma_start(x_sb[:, p], x_t[bass.ds(n, 1)].rearrange("a p t d -> p (a t) d")).then_inc(x_ld[p], 16)

            def chosen_experts():
                return [sp.value_load(chosen[0:1, i:i + 1], min_val=0, max_val=E - 1) for i in range(2)]

            def load_w1(b):
                sp.wait_ge(idx_done, b + 1)
                sp.sem_inc(stood, 1)
                e = chosen_experts()
                if not (isinstance(b, int) and b == 0):
                    sp.wait_ge(gelu_done, b * NC * 2 * KD + 2)
                for i in range(2):
                    sp.dma_start(w1e[:, i], ins["w1"][bass.ds(e[i], 1)].rearrange("a (k p) n -> p (a k) n", p=P)
                                 ).then_inc(w1_ld, 16)
                    with nc.allow_non_contiguous_dma(reason="256 words of bias"):
                        sp.dma_start(b1e[:, i], ins["b1"][bass.ds(e[i], 1)].rearrange("a (k p) -> p (a k)", p=P)
                                     ).then_inc(w1_ld, 16)

            def load_w2(b):
                sp.wait_ge(o_read, b * NC + 1)
                sp.sem_inc(stood, 1)
                e = chosen_experts()
                for i in range(2):
                    sp.dma_start(w2e[:, i], ins["w2"][bass.ds(e[i], 1)].rearrange("a (k p) n -> p (a k) n", p=P)
                                 ).then_inc(w2_ld, 16)
                    sp.dma_start(b2e[:, i], ins["b2"][bass.ds(e[i], 1)].rearrange("a d -> (a d)")
                                 .partition_broadcast(P)).then_inc(w2_ld, 16)

            def step(b, c):
                new = ahead(b, c, 4)
                if new and not (isinstance(b, int) and new[2] < 2):
                    sp.wait_ge(x1_done, new[2] - 1)
                    load_x(new[2], new[1] % 2)
                if c == NC - 1 and not (isinstance(b, int) and b == B - 1):
                    load_w1(b + 1)
                if ahead(b, c, 0):
                    if c == 0:
                        load_w2(b)
                    n = b * NC + c
                    sp.wait_ge(out_done, n + 1)
                    sp.dma_start(out_t[bass.ds(n, 1)].rearrange("a p t d -> p (a t) d"), out_sb[:, c % 2]
                                 ).then_inc(stored[c % 2], 16)

            for n in range(2):
                load_x(n, n)
            steps(sp, step)
            for p in range(2):
                sp.wait_ge(stored[p], 16 + 16 * B * NC // 2)

        @block.gpsimd
        def _(pool):
            def load_ctx(b, c):
                for k in range(KD):
                    pool.dma_start(cc[:, c % 2, k], ctx_all[:, bass.ds((b * KD + k) * NT + c * TT, TT), :]
                                 ).then_inc(cc_ld[c % 2], 16)

            def step(b, c):
                new = ahead(b, c, 4)
                if new and not (isinstance(b, int) and new[2] < 2):
                    pool.wait_ge(ctx_turned, new[2] - 1)
                    pool.sem_inc(stood, 1)
                    load_ctx(*new[:2])

            for n in range(2):
                load_ctx(0, n)
            steps(pool, step)

        @block.vector
        def _(v):
            def take_projection(b, c, n):
                v.wait_ge(a_done, n + 1)
                nc.vector.tensor_tensor(attn[:, :, :], psA[:, :, :],
                                        consts.bo[:, :].unsqueeze(1).to_broadcast([P, TT, D]), ALU.add
                                        ).then_inc(a_read, 1)
                v.wait_ge(a_read, n + 1)
                ln_a.variance(Chain(v, chain_a, n * LN_MARKS), attn, var_a)

            def add_attention(b, c, n):
                v.wait_ge(std_a, n + 1)
                ln_a.normalise(Chain(v, chain_a, n * LN_MARKS + LN_MARKS - 1), attn, attn).then_inc(norm_a, 1)
                v.wait_ge(norm_a, n + 1)
                v.wait_ge(x_ld[c % 2], (b * 2 + c // 2 + 1) * 16)
                nc.vector.tensor_tensor(x1[:, c], x_sb[:, c % 2], attn[:, :, :], ALU.add).then_inc(x1_done, 1)
                v.wait_ge(x1_done, n + 1)
                ln_x.variance(Chain(v, chain_x, n * LN_MARKS), x1[:, c], var_x)

            def normalise_x1(b, c, n):
                v.wait_ge(std_x, n + 1)
                wait_for(v, y_turned, n)
                ln_x.normalise(Chain(v, chain_x, n * LN_MARKS + LN_MARKS - 1), x1[:, c], y).then_inc(y_done, 1)

            def route(b):
                chain = Chain(v, chain_r, b * 9)
                v.wait_ge(logits, b + 1)
                chain.mark(nc.vector.tensor_tensor(rt[:, 0], psA[0:1, 0, 0:E], consts.br[:, :], ALU.add))
                for i in range(2):
                    score, equal, where = rt[:, 3 * i], rt[:, 3 * i + 1], rt[:, 3 * i + 2]
                    top, at = best[:, 2 * i:2 * i + 1], best[:, 2 * i + 1:2 * i + 2]
                    chain.wait()
                    chain.mark(nc.vector.tensor_reduce(top, score, AX.X, ALU.max))
                    chain.wait()
                    chain.mark(nc.vector.scalar_tensor_tensor(out=where, in0=score, scalar=top, in1=place[:, :],
                                                              op0=ALU.is_equal, op1=ALU.mult))
                    chain.wait()
                    chain.mark(nc.vector.tensor_reduce(at, where, AX.X, ALU.min))
                    chain.wait()
                    if i == 0:
                        chain.mark(nc.vector.tensor_scalar(equal, place[:, :], at, -3.0e38, ALU.is_equal, ALU.mult))
                        chain.wait()
                        chain.mark(nc.vector.tensor_tensor(rt[:, 3], score, equal, ALU.add))
                nc.vector.tensor_scalar(chosen[:, :], best[:, :].rearrange("o (i two) -> o i two", two=2)[:, :, 1],
                                        float(E), None, ALU.add).then_inc(idx_done, 1)

            def experts_end(b, c, n):
                p = c % 2
                if c == 0:
                    v.wait_ge(w2_ld, (b + 1) * 16 * W_LOADS)
                    nc.vector.tensor_scalar(b2half[:, :], b2e[:, 0], 0.5, None, ALU.mult).then_inc(chain_b, 1)
                    v.wait_ge(chain_b, b * 2 + 1)
                    nc.vector.scalar_tensor_tensor(out=b2mean[:, :], in0=b2e[:, 1], scalar=0.5, in1=b2half[:, :],
                                                   op0=ALU.mult, op1=ALU.add).then_inc(chain_b, 1)
                    v.wait_ge(chain_b, b * 2 + 2)
                if isinstance(b, int):
                    v.wait_ge(out_done, n)
                v.wait_ge(o_done, n + 1)
                nc.vector.scalar_tensor_tensor(out=ffn[:, :, :], in0=psO[:, :, :], scalar=0.5,
                                               in1=b2mean[:, :].unsqueeze(1).to_broadcast([P, TT, D]),
                                               op0=ALU.mult, op1=ALU.add).then_inc(o_read, 1)
                v.wait_ge(o_read, n + 1 + 1)
                chain = Chain(v, chain_f, n * LN_MARKS)
                ln_f.variance(chain, ffn, var_f)
                v.wait_ge(std_f, n + 1)
                ln_f.normalise(chain, ffn, ffn).then_inc(norm_f, 1)
                v.wait_ge(norm_f, n + 1)
                v.wait_ge(stored[p], 16 + (b * 2 + c // 2) * 16)
                nc.vector.tensor_tensor(out_sb[:, p], x1[:, c], ffn[:, :, :], ALU.add).then_inc(out_done, 1)

            def step(b, c):
                for k, part in ((2, normalise_x1), (3, add_attention), (4, take_projection), (0, experts_end)):
                    which = ahead(b, c, k)
                    if which:
                        part(*which)
                turned = ahead(b, c, 2)
                if turned and turned[1] == 0:
                    route(turned[0])

            v.wait_ge(consts.set, consts.BUILT)
            v.wait_ge(consts.loaded, 16 * consts.LOADS)
            v.sem_inc(o_read, 1)
            for p in range(2):
                v.sem_inc(stored[p], 16)
            steps(v, step)

        @block.scalar
        def _(act):
            def copy_ctx(b, c, n):
                act.wait_ge(ctx_turned, n + 1)
                nc.scalar.copy(ccT[:, :, :], psT[:, :, :]).then_inc(ccT_done, 1)

            def gelu(b, c, n):
                if c == 0:
                    act.wait_ge(w1_ld, (b + 1) * 16 * W_LOADS)
                for i in range(2 * KD):
                    e, m = divmod(i, KD)
                    act.wait_ge(h_done, n * 2 * KD + i + 1)
                    nc.scalar.activation(hT[:, e, m], psH[:, i % 2], ACT.Gelu, bias=b1e[:, e, m:m + 1]
                                         ).then_inc(gelu_done, 1)

            def root_x1(b, c, n):
                act.wait_ge(var_x, n + 1)
                ln_x.root(consts.eps, std_x)

            def copy_y(b, c, n):
                act.wait_ge(y_turned, n + 1)
                nc.scalar.copy(yT[:, :, c], psT[:, :, :]).then_inc(yT_done, 1)

            def root_attn(b, c, n):
                act.wait_ge(var_a, n + 1)
                ln_a.root(consts.eps, std_a)

            def root_ffn(b, c, n):
                act.wait_ge(var_f, n + 1)
                ln_f.root(consts.eps, std_f)

            def step(b, c):
                for k, part in ((4, copy_ctx), (0, gelu), (3, root_x1), (2, copy_y), (4, root_attn), (0, root_ffn)):
                    which = ahead(b, c, k)
                    if which:
                        part(*which)

            act.sem_inc(gelu_done, 2)
            steps(act, step)

        @block.tensor
        def _(pe):
            def turn_ctx(b, c, n):
                wait_for(pe, yT_done, n - 2)
                pe.wait_ge(cc_ld[c % 2], (b * 2 + c // 2 + 1) * 16 * KD)
                for k in range(KD):
                    for t in range(TT):
                        ins_ = nc.tensor.transpose(psT[:, k, t * P:(t + 1) * P], cc[:, c % 2, k, t], ident[:, :])
                ins_.then_inc(ctx_turned, 1)

            def project(b, c, n):
                pe.wait_ge(ccT_done, n + 1)
                wait_for(pe, a_read, n)
                if c == 3:
                    pe.wait_ge(idx_done, b + 1)
                for t in range(TT):
                    for k in range(KD):
                        ins_ = nc.tensor.matmul(psA[:, t], ccT[:, k, t * P:(t + 1) * P], wo[:, k],
                                                start=(k == 0), stop=(k == KD - 1))
                ins_.then_inc(a_done, 1)

            def turn_y(b, c, n):
                pe.wait_ge(y_done, n + 1)
                for k in range(KD):
                    for t in range(TT):
                        ins_ = nc.tensor.transpose(psT[:, k, t * P:(t + 1) * P], y[:, t, k * P:(k + 1) * P],
                                                   ident[:, :])
                ins_.then_inc(y_turned, 1)

            def score_experts(b, n):
                pe.wait_ge(yT_done, n + 1)
                pe.wait_ge(a_read, n + 3)
                for k in range(KD):
                    ins_ = nc.tensor.matmul(psA[0:1, 0, 0:E], yT[:, k, 0, 0:1], wr[:, k],
                                            start=(k == 0), stop=(k == KD - 1))
                ins_.then_inc(logits, 1)

            def hidden(b, c, n):
                if c == 0:
                    pe.wait_ge(w1_ld, (b + 1) * 16 * W_LOADS)
                pe.wait_ge(yT_done, n + 1)
                for i in range(2 * KD):
                    e, m = divmod(i, KD)
                    pe.wait_ge(gelu_done, n * 2 * KD + i - 1 + 2)
                    for k in range(KD):
                        ins_ = nc.tensor.matmul(psH[:, i % 2], w1e[:, e, k, m * P:(m + 1) * P], yT[:, k, c],
                                                start=(k == 0), stop=(k == KD - 1))
                    ins_.then_inc(h_done, 1)

            def outer(b, c, n):
                if c == 0:
                    pe.wait_ge(w2_ld, (b + 1) * 16 * W_LOADS)
                pe.wait_ge(gelu_done, (n + 1) * 2 * KD + 2)
                pe.wait_ge(o_read, n + 1)
                for t in range(TT):
                    for i in range(2 * KD):
                        e, m = divmod(i, KD)
                        ins_ = nc.tensor.matmul(psO[:, t], hT[:, e, m, t * P:(t + 1) * P], w2e[:, e, m],
                                                start=(i == 0), stop=(i == 2 * KD - 1))
                ins_.then_inc(o_done, 1)

            def step(b, c):
                for k, part in ((4, turn_ctx), (0, hidden), (4, project), (2, turn_y), (0, outer)):
                    which = ahead(b, c, k)
                    if which:
                        part(*which)
                turned = ahead(b, c, 2)
                if turned and turned[1] == 0:
                    score_experts(turned[0], turned[2])

            pe.wait_ge(consts.loaded, 16 * consts.LOADS)
            steps(pe, step)


def program(nc, ins, out):
    qk_scr = nc.dram_tensor("qk_parts", (2, 3, B * D, S), BF16, kind="Internal").ap()
    v_scr = nc.dram_tensor("v_ones", (B * NG, S, HG * VW), F32, kind="Internal").ap()
    with ExitStack() as outer:
        shared = outer.enter_context(nc.sbuf_tensor("shared", [P, B * KD * NT * P], F32))
        ctx_all = shared[:, :].rearrange("p (n d) -> p n d", d=P)
        consts = Constants(nc, outer)
        with ExitStack() as ctx:
            groups = Groups(nc, ctx, qk_scr, v_scr)
            stage_a(nc, ins, qk_scr, v_scr, consts, groups, shared)
            stage_b(nc, consts, groups, ctx_all)
        stage_c(nc, ins, consts, ctx_all, out)




_NAMES = {"x": "L0_attn_x", "wq": "L0_attn_wq", "bq": "L0_attn_bq", "wk": "L0_attn_wk", "bk": "L0_attn_bk",
          "wv": "L0_attn_wv", "bv": "L0_attn_bv", "wo": "L0_attn_wo", "bo": "L0_attn_bo", "wr": "L0_ffn_Wr",
          "br": "L0_ffn_br", "w1": "L0_ffn_W1", "b1": "L0_ffn_b1", "w2": "L0_ffn_W2", "b2": "L0_ffn_b2"}


def kernel(**inputs):
    import numpy as _np
    import concourse.bacc as _bacc
    from concourse import mybir as _mybir
    from concourse.bass_utils import run_bass_kernel_spmd as _run

    nc = _bacc.Bacc("TRN2", target_bir_lowering=False, num_devices=1)
    arrays, aps = {}, {}
    for short, name in _NAMES.items():
        a = _np.ascontiguousarray(inputs[name])
        arrays[f"in_{name}"] = a
        aps[short] = nc.dram_tensor(f"in_{name}", a.shape, _mybir.dt.from_np(a.dtype), kind="ExternalInput").ap()
    out = nc.dram_tensor("out_0", (B, S, D), F32, kind="ExternalOutput").ap()
    program(nc, aps, out)
    r = _run(nc, [arrays], core_ids=[0])
    return r.results[0]["out_0"]
```

```python
from contextlib import ExitStack

import concourse.bass as bass
from concourse import mybir

F32 = mybir.dt.float32
BF16 = mybir.dt.bfloat16
I32 = mybir.dt.int32
ALU = mybir.AluOpType
ACT = mybir.ActivationFunctionType
AX = mybir.AxisListType

P = 128
B, S, D = 4, 2048, 256
H, HD = 16, 16
E = 8
KD = D // P
CH = 512
TT = CH // P
NC = S // CH
NT = S // P
HG = 4
NG = H // HG
VW = 32
EPS = 1e-5
SCALE = float(HD) ** -0.5
NEG = -1e30

SLOTS = [(0, 0), (0, 1), (1, 0), (0, 2), (1, 1), (2, 0)]
KR = HD * len(SLOTS)


class Chain:

    def __init__(self, eng, sem, base):
        self.eng, self.sem, self.base, self.n = eng, sem, base, 0

    def mark(self, ins):
        self.n += 1
        ins.then_inc(self.sem, 1)

    def wait(self):
        self.eng.wait_ge(self.sem, self.base + self.n)


LN_MARKS = 4


class LayerNorm:

    def __init__(self, nc, sb, name):
        self.nc = nc
        self.stats = sb(name + "_stats", [P, TT, 6], F32)
        self.tmp = sb(name + "_tmp", [P, 4, TT], F32)
        self.mean = sb(name + "_mean", [P, TT], F32)
        self.var = sb(name + "_var", [P, TT], F32)
        self.std = sb(name + "_std", [P, TT], F32)
        self.rstd = sb(name + "_rstd", [P, TT], F32)

    def variance(self, chain, src, var_done):
        v, st, tmp = self.nc.vector, self.stats, self.tmp
        for t in range(TT):
            last = v.bn_stats(st[:, t, :], src[:, t])
        chain.mark(last)
        chain.wait()
        v.tensor_tensor(tmp[:, 0, :], st[:, :, 1], st[:, :, 4], ALU.subtract)
        v.tensor_tensor(tmp[:, 1, :], st[:, :, 2], st[:, :, 5], ALU.add)
        chain.mark(v.tensor_tensor(tmp[:, 2, :], st[:, :, 1], st[:, :, 4], ALU.add))
        chain.wait()
        v.scalar_tensor_tensor(out=tmp[:, 3, :], in0=tmp[:, 0, :], scalar=float(D // 4), in1=tmp[:, 0, :],
                               op0=ALU.mult, op1=ALU.mult)
        chain.mark(v.tensor_scalar(self.mean[:, :], tmp[:, 2, :], 0.5, None, ALU.mult))
        chain.wait()
        v.tensor_tensor(self.var[:, :], tmp[:, 3, :], tmp[:, 1, :], ALU.add).then_inc(var_done, 1)

    def root(self, eps, std_done):
        self.nc.scalar.activation(self.std[:, :], self.var[:, :], ACT.Sqrt, bias=eps[:, 0:1],
                                  scale=1.0 / D).then_inc(std_done, 1)

    def normalise(self, chain, src, dst):
        v = self.nc.vector
        chain.mark(v.reciprocal(self.rstd[:, :], self.std[:, :]))
        chain.wait()
        for t in range(TT):
            last = v.tensor_scalar(dst[:, t], src[:, t], self.mean[:, t:t + 1], self.rstd[:, t:t + 1],
                                   ALU.subtract, ALU.mult)
        return last


class Constants:

    IDENT, EPS_SET, BUILT = 2, 3, 6 + E
    LOADS = 4

    def __init__(self, nc, ctx):
        def sb(name, shape, dt):
            return ctx.enter_context(nc.sbuf_tensor(name, shape, dt))

        self.nc = nc
        self.ident = sb("ident", [P, P], F32)
        self.identb = sb("identb", [P, P], BF16)
        self.above = sb("above", [P, P], BF16)
        self.eps = sb("eps", [P, 1], F32)
        self.place = sb("place", [1, E], F32)
        self.wo = sb("wo", [P, KD, D], F32)
        self.bo = sb("bo", [P, D], F32)
        self.wr = sb("wr", [P, KD, E], F32)
        self.br = sb("br", [1, E], F32)
        self.set = ctx.enter_context(nc.semaphore("const_set"))
        self.loaded = ctx.enter_context(nc.semaphore("const_loaded"))

    def build_first(self, pool):
        self.nc.gpsimd.memset(self.ident[:, :], 0.0).then_inc(self.set, 1)
        pool.wait_ge(self.set, 1)
        self.nc.gpsimd.affine_select(out=self.ident[:, :], in_=self.ident[:, :], compare_op=ALU.not_equal,
                                     fill=1.0, base=0, pattern=[[-1, P]], channel_multiplier=1
                                     ).then_inc(self.set, 1)
        self.nc.gpsimd.memset(self.eps[:, :], EPS).then_inc(self.set, 1)

    def build_rest(self, pool):
        self.nc.gpsimd.memset(self.above[:, :], 0.0).then_inc(self.set, 1)
        pool.wait_ge(self.set, 4)
        self.nc.gpsimd.tensor_copy(self.identb[:, :], self.ident[:, :]).then_inc(self.set, 1)
        self.nc.gpsimd.affine_select(out=self.above[:, :], in_=self.above[:, :], compare_op=ALU.is_ge, fill=NEG,
                                     base=0, pattern=[[-1, P]], channel_multiplier=1).then_inc(self.set, 1)
        for e in range(E):
            pool.wait_ge(self.set, 6 + e)
            self.nc.gpsimd.memset(self.place[:, e:e + 1], float(e - E)).then_inc(self.set, 1)

    def load(self, sp, ins):
        sp.dma_start(self.wo[:, :], ins["wo"].rearrange("(k p) n -> p k n", p=P)).then_inc(self.loaded, 16)
        sp.dma_start(self.wr[:, :], ins["wr"].rearrange("(k p) n -> p k n", p=P)).then_inc(self.loaded, 16)
        sp.dma_start(self.bo[:, :], ins["bo"].partition_broadcast(P)).then_inc(self.loaded, 16)
        sp.dma_start(self.br[:, :], ins["br"].unsqueeze(0)).then_inc(self.loaded, 16)


class Chunks:

    def __init__(self, nc, ctx, ins, o_scr, inv_scr):
        def sb(name, shape):
            return ctx.enter_context(nc.sbuf_tensor(name, shape, F32))

        def sem(name):
            return ctx.enter_context(nc.semaphore(name))

        self.nc, self.o_scr, self.inv_scr = nc, o_scr, inv_scr
        self.x_t = ins["x"].rearrange("b (c t p) d -> (b c) p t d", p=P, t=TT)
        self.outT = sb("b_outT", [P, 2, CH])
        self.out_stored = [sem(f"b_out_stored{p}") for p in range(2)]
        self.x_sb = sb("c_x", [P, 2, TT, D])
        self.cc = sb("c_cc", [P, NC, KD, CH])
        self.inv = sb("c_inv", [P, NC, KD, CH])
        self.pair_sums = sb("b_pair_sums", [P, 2 * HG * S // P])
        self.sums_ld = sem("b_sums_ld")
        self.sums_inv = sem("b_sums_inv")
        self.inv_stored = sem("b_inv_stored")
        self.x_ld = [sem(f"c_x_ld{p}") for p in range(2)]
        self.first_ld = sem("c_first_ld")
        self.cc_ld = [sem(f"c_cc_ld{c}") for c in range(NC)]

    def load_x(self, eng, n, p):
        eng.dma_start(self.x_sb[:, p], self.x_t[bass.ds(n, 1)].rearrange("a p t d -> p (a t) d")
                      ).then_inc(self.x_ld[p], 16)

    def load_sums(self, sp, q):
        for p in range(2):
            sp.wait_ge(self.out_stored[p], (q + 1) * NC * 16)
        if not (isinstance(q, int) and q == 0):
            sp.wait_ge(self.inv_stored, q * 16)
        sp.dma_start(self.pair_sums[:, :], self.o_scr[bass.ds(q * 2 * HG, 2 * HG), HD:HD + 1, :]
                     .rearrange("h o (a n) -> h (o a) n", n=2 * HG * S // P)).then_inc(self.sums_ld, 16)

    def invert_sums(self, v, q):
        v.wait_ge(self.sums_ld, (q + 1) * 16)
        self.nc.vector.reciprocal(self.pair_sums[:, :], self.pair_sums[:, :]).then_inc(self.sums_inv, 1)

    def store_inverses(self, sp, q):
        sp.wait_ge(self.sums_inv, q + 1)
        sp.dma_start(self.inv_scr[bass.ds(q * 2 * HG, 2 * HG), :]
                     .rearrange("h (a n) -> (h a) n", n=2 * HG * S // P), self.pair_sums[:, :]
                     ).then_inc(self.inv_stored, 16)

    def load_ctx(self, eng, b, c, done):
        for k in range(KD):
            heads = bass.ds(b * H + k * 2 * HG, 2 * HG)
            eng.dma_start(self.cc[:, c, k], self.o_scr[heads, 0:HD, c * CH:(c + 1) * CH]).then_inc(done, 16)
            eng.dma_start(self.inv[:, c, k], self.inv_scr[heads, c * CH:(c + 1) * CH].unsqueeze(1)
                          .to_broadcast([2 * HG, HD, CH])).then_inc(done, 16)

    LOADS = 4

    def load_first(self, eng):
        for c in range(NC):
            self.load_ctx(eng, 0, c, self.first_ld)
            if c < 2:
                self.load_x(eng, c, c)


class Groups:

    LOADS = 2 * len(SLOTS) + 2

    def __init__(self, nc, ctx, qk_scr, v_scr):
        self.nc, self.qk_scr, self.v_scr = nc, qk_scr, v_scr
        self.qT = ctx.enter_context(nc.sbuf_tensor("g_qT", [P, 2, HG, S], BF16))
        self.kT = ctx.enter_context(nc.sbuf_tensor("g_kT", [P, 2, HG, S], BF16))
        self.vS = ctx.enter_context(nc.sbuf_tensor("g_v", [P, 2, NT, HG * VW], F32))
        self.loaded = [ctx.enter_context(nc.semaphore(f"g_loaded{p}")) for p in range(2)]

    def write_ones(self, done):
        self.nc.gpsimd.memset(self.kT[KR:KR + 1, :, :, :], 1.0).then_inc(done, 1)

    def load(self, sp, at, g):
        for t, buf in enumerate((self.qT, self.kT)):
            for s, slot in enumerate(SLOTS):
                sp.dma_start(buf[s * HD:(s + 1) * HD, g],
                             self.qk_scr[t, slot[t], bass.ds(at * HG * HD, HG * HD), :]
                             .rearrange("(h d) n -> d h n", d=HD)).then_inc(self.loaded[g], 16)
        for t in range(0, NT, NT // 2):
            sp.dma_start(self.vS[:, g, t:t + NT // 2], self.v_scr[bass.ds(at, 1), t * P:(t + NT // 2) * P]
                         .rearrange("a (t p) n -> p (a t) n", p=P)).then_inc(self.loaded[g], 16)


def stage_a(nc, ins, qk_scr, v_scr, consts, groups, chunks):
    with ExitStack() as ctx:
        def sb(name, shape, dt):
            return ctx.enter_context(nc.sbuf_tensor(name, shape, dt))

        def pb(name, shape, dt):
            return ctx.enter_context(nc.psum_tensor(name, shape, dt))

        def sem(name):
            return ctx.enter_context(nc.semaphore(name))

        ident = consts.ident
        w = sb("a_w", [P, 3, KD, D], F32)
        bqk = sb("a_bqk", [P, 2, KD], F32)
        bqs = sb("a_bqs", [P, KD], F32)
        bvb = sb("a_bv", [P, D], F32)
        x_sb = sb("a_x", [P, 2, TT, D], F32)
        xn = sb("a_xn", [P, 2, TT, D], F32)
        xT = chunks.cc[:, 0:2]
        full, rest = (chunks.inv[:, i:i + 2].rearrange("p b k n -> p (b k) n") for i in (0, 2))
        v_sb = sb("a_v", [P, 2, TT, H * VW], F32)
        parts = sb("a_parts", [P, 2, 2 * KD, 3, CH], BF16)
        ln = LayerNorm(nc, sb, "a_ln")
        psT = pb("a_psT", [P, KD, CH], F32)
        psQK = pb("a_psQK", [P, 2 * KD, CH], F32)
        psV = pb("a_psV", [P, TT, D], F32)

        w_ld = sem("a_w_ld")
        x_ld = [sem(f"a_x_ld{p}") for p in range(2)]
        v_set = sem("a_v_set")
        b_scaled = sem("a_b_scaled")
        chain_s = sem("a_chain")
        var_done = sem("a_var_done")
        std_done = sem("a_std_done")
        xn_done = sem("a_xn_done")
        turned = sem("a_turned")
        xT_done = sem("a_xT_done")
        qk_done = sem("a_qk_done")
        full_s = sem("a_full_done")
        hi_done = sem("a_hi_done")
        rest_done = sem("a_rest_done")
        mid_done = sem("a_mid_done")
        last_v = sem("a_last_v")
        v_done = sem("a_v_done")
        chunk_done = sem("a_chunk_done")
        stored = [sem(f"a_stored{p}") for p in range(2)]
        STORES = 2 * KD + NG

        x_t = ins["x"].rearrange("b (c t p) d -> (b c) p t d", p=P, t=TT)
        block = ctx.enter_context(nc.Block())

        def portions(last, c):
            return [(0, KD), (KD, 2 * KD)] if last and c == NC - 1 else [(0, 2 * KD)]

        def batches(eng, body):
            with eng.Fori(0, B - 1) as b:
                body(b, False)
            body(B - 1, True)

        @block.sync
        def _(sp):
            sp.dma_start(x_sb[:, 0], x_t[0]).then_inc(x_ld[0], 16)
            for i, name in enumerate(("wq", "wk", "wv")):
                sp.dma_start(w[:, i], ins[name].rearrange("(k p) n -> p k n", p=P)).then_inc(w_ld, 16)
            with nc.allow_non_contiguous_dma(reason="512 words of bias"):
                for i, name in enumerate(("bq", "bk")):
                    sp.dma_start(bqk[:, i], ins[name].rearrange("(k p) -> p k", p=P)).then_inc(w_ld, 16)
            sp.dma_start(bvb[:, :], ins["bv"].partition_broadcast(P)).then_inc(w_ld, 16)
            sp.dma_start(x_sb[:, 1], x_t[1]).then_inc(x_ld[1], 16)

            def store_v(b, c):
                for g in range(NG):
                    sp.dma_start(v_scr[bass.ds(b * NG + g, 1), c * CH:(c + 1) * CH, :]
                                 .rearrange("a (t p) n -> p (a t) n", p=P),
                                 v_sb[:, c % 2, :, g * HG * VW:(g + 1) * HG * VW]).then_inc(stored[c % 2], 16)

            def body(b, last):
                for c in range(NC):
                    n = b * NC + c
                    p = c % 2
                    if not (last and c >= NC - 3):
                        sp.wait_ge(xn_done, n + 2)
                        load_x(n + 3, 1 - p)
                    if last and c == NC - 1:
                        sp.wait_ge(last_v, 1)
                        store_v(b, c)
                    for i, (lo, hi) in enumerate(portions(last, c)):
                        sp.wait_ge(chunk_done, n + 1 + 1 + i)
                        for at in range(lo, hi):
                            t, m = divmod(at, KD)
                            sp.dma_start(qk_scr[t, :, bass.ds(b * D + m * P, P), c * CH:(c + 1) * CH]
                                         .rearrange("s p n -> p s n"), parts[:, p, at]).then_inc(stored[p], 16)
                    if not (last and c == NC - 1):
                        store_v(b, c)
                    if last and c == 0:
                        for q in range(2):
                            sp.wait_ge(stored[q], 16 + 16 * STORES * NC // 2)
                        groups.load(sp, 0, 0)

            def load_x(n, p):
                sp.dma_start(x_sb[:, p], x_t[bass.ds(n, 1)].rearrange("a p t d -> p (a t) d")).then_inc(x_ld[p], 16)

            consts.load(sp, ins)
            sp.wait_ge(xn_done, 1)
            load_x(2, 0)
            batches(sp, body)
            for p in range(2):
                sp.wait_ge(stored[p], 16 + 16 * STORES * B * NC // 2)

        @block.gpsimd
        def _(pool):
            consts.build_first(pool)
            nc.gpsimd.memset(v_sb[:, :, :, :], 0.0).then_inc(v_set, 1)
            pool.wait_ge(v_set, 1)
            nc.gpsimd.memset(v_sb[:, :, :, :].rearrange("p b t (h e) -> p (b t h) e", e=VW)[:, :, HD:HD + 1],
                             1.0).then_inc(v_set, 1)
            pool.wait_ge(v_set, 2)
            groups.write_ones(v_set)
            pool.wait_ge(v_set, 3)
            consts.build_rest(pool)

        @block.vector
        def _(v):
            def variance(b, c):
                chain = Chain(v, chain_s, (b * NC + c) * LN_MARKS)
                v.wait_ge(x_ld[c % 2], (b * 2 + c // 2 + 1) * 16)
                ln.variance(chain, x_sb[:, c % 2], var_done)
                return chain

            def normalise(chain, b, c):
                v.wait_ge(std_done, b * NC + c + 1)
                ln.normalise(chain, x_sb[:, c % 2], xn[:, c % 2]).then_inc(xn_done, 1)

            def add_v(n, p):
                v.wait_ge(v_done, n + 1)
                for t in range(0, TT, 2):
                    ins_ = nc.vector.tensor_tensor(
                        v_sb[:, p, t:t + 2].rearrange("p t (h e) -> p t h e", e=VW)[:, :, :, 0:HD],
                        psV[:, t:t + 2].rearrange("p t (h e) -> p t h e", e=HD),
                        bvb[:, :].rearrange("p (h e) -> p h e", e=HD).unsqueeze(1).to_broadcast([P, 2, H, HD]),
                        ALU.add)
                return ins_

            def body(b, last):
                for c in range(NC):
                    n = b * NC + c
                    p = c % 2
                    after = (b, c + 2) if c + 2 < NC else None if last else (b + 1, c + 2 - NC)
                    if after:
                        chain = variance(*after)
                    v.wait_ge(chunk_done, n + 1)
                    if last and c == NC - 1:
                        v.wait_ge(stored[p], 16 + (b * 2 + c // 2) * 16 * STORES)
                        add_v(n, p).then_inc(last_v, 1)
                    for i, (lo, hi) in enumerate(portions(last, c)):
                        v.wait_ge(hi_done, n + 1 + i)
                        nc.vector.tensor_tensor(rest[:, lo:hi], full[:, lo:hi], parts[:, p, lo:hi, 0],
                                                ALU.subtract).then_inc(rest_done, 1)
                    if after:
                        normalise(chain, *after)
                    for i, (lo, hi) in enumerate(portions(last, c)):
                        v.wait_ge(mid_done, n + 1 + i)
                        low = nc.vector.tensor_tensor(parts[:, p, lo:hi, 2], rest[:, lo:hi], parts[:, p, lo:hi, 1],
                                                      ALU.subtract)
                        if last and c == NC - 1:
                            low.then_inc(chunk_done, 1)
                    if not (last and c == NC - 1):
                        add_v(n, p).then_inc(chunk_done, 1)

            normalise(variance(0, 0), 0, 0)
            normalise(variance(0, 1), 0, 1)
            v.wait_ge(v_set, 2)
            v.wait_ge(w_ld, 6 * 16)
            nc.vector.tensor_scalar(bqs[:, :], bqk[:, 0], SCALE, None, ALU.mult).then_inc(b_scaled, 1)
            batches(v, body)

        @block.scalar
        def _(act):
            def root(b, c):
                act.wait_ge(var_done, b * NC + c + 1)
                ln.root(consts.eps, std_done)

            def copy_xT(b, c):
                act.wait_ge(turned, b * NC + c + 1)
                nc.scalar.copy(xT[:, c % 2], psT[:, :, :]).then_inc(xT_done, 1)

            def body(b, last):
                for c in range(NC):
                    n = b * NC + c
                    p = c % 2
                    after = None if last and c == NC - 1 else (b, c + 1) if c + 1 < NC else (b + 1, 0)
                    for i in range(2 * KD):
                        act.wait_ge(qk_done, n * 2 * KD + i + 1)
                        t, m = divmod(i, KD)
                        nc.scalar.activation(full[:, i], psQK[:, i], ACT.Identity,
                                             bias=bqs[:, m:m + 1] if t == 0 else bqk[:, 1, m:m + 1],
                                             scale=SCALE if t == 0 else 1.0).then_inc(full_s, 1)
                    if after:
                        copy_xT(*after)
                    act.wait_ge(stored[p], 16 + (b * 2 + c // 2) * 16 * STORES)
                    for lo, hi in portions(last, c):
                        act.wait_ge(full_s, n * 2 * KD + hi)
                        nc.scalar.copy(parts[:, p, lo:hi, 0], full[:, lo:hi]).then_inc(hi_done, 1)
                    if c + 2 < NC:
                        root(b, c + 2)
                    elif not last:
                        root(b + 1, c + 2 - NC)
                    for i, (lo, hi) in enumerate(portions(last, c)):
                        act.wait_ge(rest_done, n + 1 + i)
                        nc.scalar.copy(parts[:, p, lo:hi, 1], rest[:, lo:hi]).then_inc(mid_done, 1)

            act.wait_ge(consts.set, consts.EPS_SET)
            for p in range(2):
                act.sem_inc(stored[p], 16)
            root(0, 0)
            root(0, 1)
            copy_xT(0, 0)
            act.wait_ge(b_scaled, 1)
            batches(act, body)

        @block.tensor
        def _(pe):
            def turn(b, c):
                pe.wait_ge(xn_done, b * NC + c + 1)
                for k in range(KD):
                    for t in range(TT):
                        ins_ = nc.tensor.transpose(psT[:, k, t * P:(t + 1) * P], xn[:, c % 2, t, k * P:(k + 1) * P],
                                                   ident[:, :])
                ins_.then_inc(turned, 1)

            def body(b, last):
                for c in range(NC):
                    n = b * NC + c
                    p = c % 2
                    pe.wait_ge(xT_done, n + 1)
                    for i in range(2 * KD):
                        t, m = divmod(i, KD)
                        for k in range(KD):
                            ins_ = nc.tensor.matmul(psQK[:, i], w[:, t, k, m * P:(m + 1) * P], xT[:, p, k],
                                                    start=(k == 0), stop=(k == KD - 1))
                        ins_.then_inc(qk_done, 1)
                    if c + 1 < NC:
                        turn(b, c + 1)
                    elif not last:
                        turn(b + 1, 0)
                    pe.wait_ge(chunk_done, n + 1)
                    for t in range(TT):
                        for k in range(KD):
                            ins_ = nc.tensor.matmul(psV[:, t], xT[:, p, k, t * P:(t + 1) * P], w[:, 2, k],
                                                    start=(k == 0), stop=(k == KD - 1))
                    ins_.then_inc(v_done, 1)

            pe.wait_ge(consts.set, consts.IDENT)
            pe.wait_ge(w_ld, 6 * 16)
            pe.sem_inc(chunk_done, 1)
            turn(0, 0)
            batches(pe, body)



GK = sum(TT * (c + 1) for c in range(NC))
BK = 2 * GK
KEY_STEPS = [(g, c, kt) for g in range(2) for c in range(NC) for kt in range(TT * (c + 1))]
PV_LAG = 2
BANKS = 3
PBUF = 4
NPAIR = B * NG // 2
CHUNKS = 2 * NC
SLOTS_OF_STEP = 3


def max_jobs():
    jobs = []
    for g in range(2):
        for c in range(NC):
            for qt in range(TT):
                for pc in range(c + 1):
                    together = 1 if pc < c else min(HG, TT // (qt + 1))
                    for h in range(0, HG, together):
                        jobs.append(["max", 0, g, c, qt, pc, range(h, h + together), False])
            jobs[-1][-1] = True
    ends = [i for i, job in enumerate(jobs) if job[-1]]
    out = []
    for i in range(len(jobs)):
        out.append(tuple(jobs[i]))
        if i - 2 in ends:
            out.append(("turn_max", 0, *jobs[i - 2][2:4]))
        if i == 1:
            out.append(("turn_max", -1, 1, NC - 1))
    return out


MAX_JOBS = max_jobs()


def width(c, qt, pc):
    return min(CH, (TT * c + qt + 1) * P - pc * CH)


def dve_cost(job):
    return 200 if job[0] == "turn_max" else 70 + len(job[6]) * width(*job[3:6])


def pe_cost(job):
    return P * 4 if job[0] == "turn_max" else len(job[6]) * (width(*job[3:6]) + P * (job[5] == job[3]))


def step_cost(j):
    cols = [0, 0]
    for i, s in enumerate((j, j - PV_LAG)):
        if 0 <= s < BK:
            _, c, kt = KEY_STEPS[s]
            cols[i] = CH - max(0, kt - TT * c) * P
    return [2 * cols[0], 2 * cols[0], 4 * cols[1]]


def ends_chunk(s):
    return s + 1 == BK or KEY_STEPS[s + 1][:2] != KEY_STEPS[s][:2]


def pair_jobs(done, until, even=None):
    jobs = [MAX_JOBS[i % len(MAX_JOBS)] for i in range(done, until)]
    jobs = [(x[0], x[1] + i // len(MAX_JOBS), *x[2:]) for i, x in enumerate(jobs, done)]
    if until == len(MAX_JOBS):
        jobs.append(("turn_max", 0, 1, NC - 1))
    rate = (sum(map(dve_cost, MAX_JOBS))
            / (sum(sum(step_cost(j)) for j in range(BK)) + sum(map(pe_cost, MAX_JOBS))))
    now = spent = 0.0
    steps = []
    for j in range(BK + PV_LAG):
        slots = [[], [], []]
        for s, cost in enumerate(step_cost(j)):
            now += cost
            while jobs and (spent < rate * now or (j == BK + 1 and s == 2)
                            or even and spent < QUICK * rate * now):
                if even and len(jobs) <= left(even, j, s):
                    break
                job = jobs.pop(0)
                spent += dve_cost(job)
                now += pe_cost(job)
                slots[s].append(job)
        steps.append(slots)
    return steps


def left(steps, j, s):
    slots = sum(steps[j + 1:], steps[j][s + 1:])
    return sum(map(len, slots))


QUICK = 1.2
SUMS_AT = 4
MARGIN = 4


def in_time(steps):
    return all(job[1] * BK + KEY_STEPS.index((job[2], job[3], 0)) >= j + MARGIN
               for j, slots in enumerate(steps) for slot in slots for job in slot if job[0] == "turn_max")


LEAD = next(n for n in range(len(MAX_JOBS)) if in_time(pair_jobs(n, n + len(MAX_JOBS))))
N_LEAD = sum(x[1] == 0 for x in MAX_JOBS[:LEAD])
BODY_JOBS = pair_jobs(LEAD, LEAD + len(MAX_JOBS))
FIRST = next(n for n in range(LEAD + 1) if in_time(pair_jobs(n, LEAD + len(MAX_JOBS), BODY_JOBS)))
FIRST_JOBS = pair_jobs(FIRST, LEAD + len(MAX_JOBS), BODY_JOBS)
LEAD_JOBS = [x for x in MAX_JOBS[:FIRST] if x[1] == 0]
LAST_JOBS = pair_jobs(LEAD, len(MAX_JOBS))
N_BODY = sum(len(slot) for slots in BODY_JOBS for slot in slots)
assert N_BODY % BANKS == 0 and BK % PBUF == 0


def stage_b(nc, consts, groups, chunks):
    with ExitStack() as ctx:
        def sb(name, shape, dt):
            return ctx.enter_context(nc.sbuf_tensor(name, shape, dt))

        def pb(name, shape, dt):
            return ctx.enter_context(nc.psum_tensor(name, shape, dt))

        def sem(name):
            return ctx.enter_context(nc.semaphore(name))

        ident, identb, above = consts.ident, consts.identb, consts.above
        qT, kT, vS, loaded = groups.qT, groups.kT, groups.vS, groups.loaded
        prob = sb("b_prob", [P, PBUF, HG, CH], F32)
        pmax = sb("b_pmax", [P, 2, HG * TT, NC], F32)
        nmax = sb("b_nmax", [P, 2, HG * TT], F32)
        nmT = sb("b_nmT", [HG * TT, 2, P], BF16)
        outT, out_stored = chunks.outT, chunks.out_stored
        psS = pb("b_psS", [P, HG, CH], F32)
        ring = pb("b_ring", [P, BANKS, CH], F32)
        psO = pb("b_psO", [P, CH], F32)

        nm_ld = [[sem(f"b_nm{p}{c}") for c in range(NC)] for p in range(2)]
        ring_full = sem("b_ring_full")
        ring_free = sem("b_ring_free")
        nm_done = sem("b_nm_done")
        scored = sem("b_scored")
        exp_done = sem("b_exp_done")
        stood = sem("b_stood")
        masked = sem("b_masked")
        pv_done = sem("b_pv_done")
        out_copied = sem("b_out_copied")
        LOADS = Groups.LOADS

        block = ctx.enter_context(nc.Block())

        def pairs(eng, body):
            body(0, FIRST_JOBS, False)
            with eng.Fori(1, NPAIR - 1) as it:
                body(it, BODY_JOBS, False)
            body(NPAIR - 1, LAST_JOBS, True)

        def chunk_index(it, g, c):
            return it * CHUNKS + g * NC + c

        @block.sync
        def _(sp):
            def place_max(q, g, c, r):
                sp.wait_ge(ring_free, r + 1)
                for h in range(HG):
                    sp.dma_start(qT[KR:KR + 1, g % 2, h, c * CH:(c + 1) * CH].rearrange("o (q n) -> o q n", n=P),
                                 nmT[h * TT:(h + 1) * TT, c % 2, :]).then_inc(nm_ld[g % 2][c], 16)

            def store_out(it, g, c):
                sp.wait_ge(out_copied, chunk_index(it, g, c) + 1 + 1)
                sp.dma_start(chunks.o_scr[bass.ds(it * 2 * HG + g * HG, HG), :, c * CH:(c + 1) * CH]
                             .rearrange("h e n -> (h e) n"), outT[:, c % 2]).then_inc(out_stored[c % 2], 16)

            def body(it, steps, last):
                i = len(LEAD_JOBS) if steps is FIRST_JOBS else N_LEAD
                for j, slots in enumerate(steps):
                    for job in sum(slots, []):
                        if job[0] == "turn_max":
                            place_max(*job[1:], it * N_BODY + i)
                        i += 1
                    if j == SUMS_AT and steps is not FIRST_JOBS:
                        chunks.load_sums(sp, it - 1)
                    if j == SUMS_AT + 8 and steps is not FIRST_JOBS:
                        chunks.store_inverses(sp, it - 1)
                    if j > PV_LAG and ends_chunk(j - PV_LAG - 1):
                        store_out(it, *KEY_STEPS[j - PV_LAG - 1][:2])
                    if j == BK - 8 and last:
                        sp.wait_ge(chunks.inv_stored, 16 * (NPAIR - 1))
                        chunks.load_first(sp)
                    if j == GK + PV_LAG + 1 and not last:
                        sp.wait_ge(pv_done, it * BK + GK + PBUF)
                        groups.load(sp, it * 2 + 2, 0)
                store_out(it, 1, NC - 1)
                if not last:
                    sp.wait_ge(pv_done, it * BK + BK + PBUF)
                    groups.load(sp, it * 2 + 3, 1)

            groups.load(sp, 1, 1)
            for r, job in enumerate(LEAD_JOBS):
                if job[0] == "turn_max":
                    place_max(*job[1:], r)
            pairs(sp, body)

        @block.gpsimd
        def _(pool):
            def body(it, steps, last):
                for j, (g, c, kt) in enumerate(KEY_STEPS):
                    i = kt - TT * c
                    if i >= 0:
                        pool.wait_ge(exp_done, it * 2 * BK + 2 * (j + 1) + 2)
                        pool.sem_inc(stood, 1)
                        tile = prob[:, j % PBUF, :, i * P:(i + 1) * P]
                        nc.gpsimd.affine_select(out=tile, in_=tile, compare_op=ALU.is_ge, fill=0.0, base=0,
                                                pattern=[[0, HG], [1, P]], channel_multiplier=-1
                                                ).then_inc(masked, 1)

            pairs(pool, body)

        @block.vector
        def _(v):
            def do(job, r, bank, it):
                if job[0] == "max":
                    _, q, g, c, qt, pc, heads, ends = job
                    k = len(heads)
                    w = width(c, qt, pc)
                    v.wait_ge(ring_full, r + 1)
                    nc.vector.tensor_reduce(
                        pmax[:, c % 2].rearrange("p (h t) n -> p h t n", t=TT)[:, heads[0]:heads[0] + k, qt, pc],
                        ring[:, bank, 0:k * w].rearrange("p (k w) -> p k w", k=k), AX.X, ALU.max).then_inc(ring_free, 1)
                    if ends:
                        v.wait_ge(ring_free, r + 1)
                        nc.vector.tensor_reduce(nmax[:, c % 2], pmax[:, c % 2, :, 0:c + 1], AX.X, ALU.max,
                                                negate=True).then_inc(nm_done, 1)
                else:
                    _, q, g, c = job
                    v.wait_ge(ring_full, r + 1)
                    bg, bc = (g, c - 2) if c >= 2 else (1 - g, c + 2)
                    count = (it + q + (0 if c < 2 and g == 0 else 1)) * 16 * HG
                    if not (isinstance(count, int) and count == 0):
                        v.wait_ge(nm_ld[bg][bc], count)
                    nc.vector.tensor_copy(nmT[:, c % 2], ring[0:HG * TT, bank, 0:P]).then_inc(ring_free, 1)

            def body(it, steps, last):
                i = len(LEAD_JOBS) if steps is FIRST_JOBS else N_LEAD
                for j, slots in enumerate(steps):
                    if j == SUMS_AT + 4 and steps is not FIRST_JOBS:
                        chunks.invert_sums(v, it - 1)
                    for job in sum(slots, []):
                        do(job, it * N_BODY + i, i % BANKS, it)
                        i += 1

            for r, job in enumerate(LEAD_JOBS):
                do(job, r, r % BANKS, 0)
            pairs(v, body)

        @block.scalar
        def _(act):
            def body(it, steps, last):
                for j in range(BK + PV_LAG):
                    if j < BK:
                        g, c, kt = KEY_STEPS[j]
                        off = max(0, kt - TT * c) * P
                        act.wait_ge(pv_done, it * BK + j + 1 - PBUF + PBUF)
                        for s in range(2):
                            act.wait_ge(scored, it * 2 * BK + 2 * j + s + 1)
                            nc.scalar.activation(prob[:, j % PBUF, 2 * s:2 * s + 2, off:CH],
                                                 psS[:, 2 * s:2 * s + 2, off:CH], ACT.Exp).then_inc(exp_done, 1)
                    s = j - PV_LAG
                    if s >= 0 and ends_chunk(s):
                        g, c, _ = KEY_STEPS[s]
                        act.wait_ge(pv_done, it * BK + s + 1 + PBUF)
                        before = it * CHUNKS // 2 + g * NC // 2 + c // 2
                        if not (isinstance(before, int) and before == 0):
                            act.wait_ge(out_stored[c % 2], before * 16)
                        nc.scalar.copy(outT[:, c % 2], psO[:, :]).then_inc(out_copied, 1)

            act.sem_inc(exp_done, 2)
            act.sem_inc(out_copied, 1)
            pairs(act, body)

        @block.tensor
        def _(pe):
            def do(job, r, bank, it):
                if not (isinstance(r, int) and r < BANKS):
                    pe.wait_ge(ring_free, r + 1 - BANKS)
                if job[0] == "max":
                    _, q, g, c, qt, pc, heads, ends = job
                    t = TT * c + qt
                    w = width(c, qt, pc)
                    if c == qt == pc == heads[0] == 0:
                        pe.wait_ge(loaded[g], (it + q + 1) * 16 * LOADS)
                    for i, h in enumerate(heads):
                        ins_ = nc.tensor.matmul(ring[:, bank, i * w:(i + 1) * w], qT[0:KR, g, h, t * P:(t + 1) * P],
                                                kT[0:KR, g, h, pc * CH:pc * CH + w], start=True, stop=pc < c)
                        if pc == c:
                            ins_ = nc.tensor.matmul(ring[:, bank, (i + 1) * w - P:(i + 1) * w], identb[:, :],
                                                    above[:, :], start=False, stop=True)
                    ins_.then_inc(ring_full, 1)
                else:
                    _, q, g, c = job
                    pe.wait_ge(nm_done, chunk_index(it + q, g, c) + 1)
                    nc.tensor.transpose(ring[0:HG * TT, bank, 0:P], nmax[:, c % 2], ident[:, :]
                                        ).then_inc(ring_full, 1)

            def body(it, steps, last):
                i = len(LEAD_JOBS) if steps is FIRST_JOBS else N_LEAD
                for j, slots in enumerate(steps):
                    for s in range(SLOTS_OF_STEP):
                        if s < 2 and j < BK:
                            g, c, kt = KEY_STEPS[j]
                            off = max(0, kt - TT * c) * P
                            if kt == 0 and s == 0:
                                pe.wait_ge(nm_ld[g][c], (it + 1) * 16 * HG)
                            pe.wait_ge(exp_done, it * 2 * BK + 2 * j + s - 1 + 2)
                            for h in (2 * s, 2 * s + 1):
                                ins_ = nc.tensor.matmul(psS[:, h, off:CH], kT[0:KR + 1, g, h, kt * P:(kt + 1) * P],
                                                        qT[0:KR + 1, g, h, c * CH + off:(c + 1) * CH],
                                                        start=True, stop=True)
                            ins_.then_inc(scored, 1)
                        jj = j - PV_LAG
                        if s == 2 and 0 <= jj < BK:
                            g, c, kt = KEY_STEPS[jj]
                            off = max(0, kt - TT * c) * P
                            if kt >= TT * c:
                                diag = sum(1 for (_, c2, k2) in KEY_STEPS[:jj + 1] if k2 >= TT * c2)
                                pe.wait_ge(masked, it * (2 * NT) + diag)
                            else:
                                pe.wait_ge(exp_done, it * 2 * BK + 2 * (jj + 1) + 2)
                            if kt == 0:
                                pe.wait_ge(out_copied, chunk_index(it, g, c) + 1)
                            for h in range(HG):
                                ins_ = nc.tensor.matmul(psO[h * VW:(h + 1) * VW, off:CH],
                                                        vS[:, g, kt, h * VW:(h + 1) * VW],
                                                        prob[:, jj % PBUF, h, off:CH],
                                                        start=(kt == 0), stop=(kt == TT * (c + 1) - 1))
                            ins_.then_inc(pv_done, 1)
                        for job in slots[s]:
                            do(job, it * N_BODY + i, i % BANKS, it)
                            i += 1

            pe.wait_ge(consts.set, consts.BUILT)
            pe.sem_inc(pv_done, PBUF)
            for r, job in enumerate(LEAD_JOBS):
                do(job, r, r % BANKS, 0)
            pairs(pe, body)


def wait_for(eng, sem, count):
    if not (isinstance(count, int) and count <= 0):
        eng.wait_ge(sem, count)


def stage_c(nc, ins, consts, chunks, out):
    with ExitStack() as ctx:
        def sb(name, shape, dt):
            return ctx.enter_context(nc.sbuf_tensor(name, shape, dt))

        def pb(name, shape, dt):
            return ctx.enter_context(nc.psum_tensor(name, shape, dt))

        def sem(name):
            return ctx.enter_context(nc.semaphore(name))

        ident, wo, wr, place = consts.ident, consts.wo, consts.wr, consts.place
        x_sb, cc, inv, x_ld, cc_ld = chunks.x_sb, chunks.cc, chunks.inv, chunks.x_ld, chunks.cc_ld
        attn = sb("c_attn", [P, TT, D], F32)
        x1 = sb("c_x1", [P, NC, TT, D], F32)
        y = sb("c_y", [P, TT, D], F32)
        yT = sb("c_yT", [P, KD, NC, CH], F32)
        w1e = sb("c_w1e", [P, 2, KD, D], F32)
        w2e = sb("c_w2e", [P, 2, KD, D], F32)
        b1e = sb("c_b1e", [P, 2, KD], F32)
        b2e = sb("c_b2e", [P, 2, D], F32)
        b2half = sb("c_b2half", [P, D], F32)
        b2mean = sb("c_b2mean", [P, D], F32)
        hT = sb("c_hT", [P, 2, KD, CH], F32)
        ffn = sb("c_ffn", [P, TT, D], F32)
        out_sb = sb("c_out", [P, 2, TT, D], F32)
        rt = sb("c_rt", [1, 6, E], F32)
        best = sb("c_best", [1, 4], F32)
        chosen = sb("c_chosen", [1, 2], I32)
        ln_a = LayerNorm(nc, sb, "c_ln_a")
        ln_x = LayerNorm(nc, sb, "c_ln_x")
        ln_f = LayerNorm(nc, sb, "c_ln_f")
        psT = pb("c_psT", [P, KD, CH], F32)
        psA = pb("c_psA", [P, TT, D], F32)
        psH = pb("c_psH", [P, 2, CH], F32)
        psO = pb("c_psO", [P, TT, D], F32)

        cc_done = sem("c_cc_done")
        a_done = sem("c_a_done")
        a_read = sem("c_a_read")
        chain_a, chain_x, chain_f = sem("c_chain_a"), sem("c_chain_x"), sem("c_chain_f")
        var_a, var_x, var_f = sem("c_var_a"), sem("c_var_x"), sem("c_var_f")
        std_a, std_x, std_f = sem("c_std_a"), sem("c_std_x"), sem("c_std_f")
        norm_a = sem("c_norm_a")
        x1_done = sem("c_x1_done")
        y_done = sem("c_y_done")
        y_turned = sem("c_y_turned")
        yT_done = sem("c_yT_done")
        logits = sem("c_logits")
        chain_r = sem("c_chain_r")
        idx_done = sem("c_idx_done")
        stood = sem("c_stood")
        w1_ld = sem("c_w1_ld")
        w2_ld = sem("c_w2_ld")
        h_done = sem("c_h_done")
        gelu_done = sem("c_gelu_done")
        o_done = sem("c_o_done")
        o_read = sem("c_o_read")
        chain_b = sem("c_chain_b")
        norm_f = sem("c_norm_f")
        out_done = sem("c_out_done")
        stored = [sem(f"c_stored{p}") for p in range(2)]
        W_LOADS = 4

        out_t = out.rearrange("b (c t p) d -> (b c) p t d", p=P, t=TT)
        block = ctx.enter_context(nc.Block())

        def ahead(b, c, k):
            b, c = b + (c + k) // NC, (c + k) % NC
            n = b * NC + c
            return None if isinstance(n, int) and not 0 <= n < B * NC else (b, c, n)

        def steps(eng, step):
            for c in range(NC):
                step(-1, c)
            with eng.Fori(0, B - 1) as b:
                for c in range(NC):
                    step(b, c)
            for c in range(NC):
                step(B - 1, c)

        def to_route(b, c):
            if isinstance(b, int) and b == -1:
                return 0 if c == NC - 2 else None
            return b + 1 if c == NC - 1 and not (isinstance(b, int) and b == B - 1) else None

        @block.sync
        def _(sp):
            def load_experts(b):
                sp.wait_ge(idx_done, b + 1)
                sp.sem_inc(stood, 1)
                e = [sp.value_load(chosen[0:1, i:i + 1], min_val=0, max_val=E - 1) for i in range(2)]
                if not (isinstance(b, int) and b == 0):
                    sp.wait_ge(gelu_done, b * NC * 2 * KD + 2)
                for i in range(2):
                    sp.dma_start(w1e[:, i], ins["w1"][bass.ds(e[i], 1)].rearrange("a (k p) n -> p (a k) n", p=P)
                                 ).then_inc(w1_ld, 16)
                    with nc.allow_non_contiguous_dma(reason="256 words of bias"):
                        sp.dma_start(b1e[:, i], ins["b1"][bass.ds(e[i], 1)].rearrange("a (k p) -> p (a k)", p=P)
                                     ).then_inc(w1_ld, 16)
                sp.wait_ge(o_read, b * NC + 1)
                for i in range(2):
                    sp.dma_start(w2e[:, i], ins["w2"][bass.ds(e[i], 1)].rearrange("a (k p) n -> p (a k) n", p=P)
                                 ).then_inc(w2_ld, 16)
                    sp.dma_start(b2e[:, i], ins["b2"][bass.ds(e[i], 1)].rearrange("a d -> (a d)")
                                 .partition_broadcast(P)).then_inc(w2_ld, 16)

            def step(b, c):
                new = ahead(b, c, 4)
                if isinstance(b, int) and b == -1 and c == 1:
                    chunks.store_inverses(sp, NPAIR - 1)
                if new and not (isinstance(b, int) and new[2] < 2):
                    sp.wait_ge(x1_done, new[2] - 1)
                    chunks.load_x(sp, new[2], new[1] % 2)
                if to_route(b, c) is not None:
                    load_experts(to_route(b, c))
                if ahead(b, c, 0):
                    n = b * NC + c
                    sp.wait_ge(out_done, n + 1)
                    sp.dma_start(out_t[bass.ds(n, 1)].rearrange("a p t d -> p (a t) d"), out_sb[:, c % 2]
                                 ).then_inc(stored[c % 2], 16)

            chunks.load_sums(sp, NPAIR - 1)
            steps(sp, step)
            for p in range(2):
                sp.wait_ge(stored[p], 16 + 16 * B * NC // 2)

        @block.gpsimd
        def _(pool):
            def step(b, c):
                new = ahead(b, c, 4)
                if new:
                    b, c, n = new
                    if not (isinstance(n, int) and n < NC):
                        pool.wait_ge(a_done, n + 1 - NC)
                        if c == 0:
                            pool.wait_ge(chunks.inv_stored, 16 * NPAIR)
                        pool.sem_inc(stood, 1)
                        chunks.load_ctx(pool, b, c, cc_ld[c])
                    if isinstance(n, int) and n < NC:
                        pool.wait_ge(chunks.first_ld, NC * 16 * chunks.LOADS)
                    else:
                        pool.wait_ge(cc_ld[c], b * 16 * chunks.LOADS)
                    pool.sem_inc(stood, 1)
                    nc.gpsimd.tensor_tensor(cc[:, c], cc[:, c], inv[:, c], ALU.mult
                                            ).then_inc(cc_done, 1)

            steps(pool, step)

        @block.vector
        def _(v):
            def take_projection(b, c, n):
                v.wait_ge(a_done, n + 1)
                nc.vector.tensor_tensor(attn[:, :, :], psA[:, :, :],
                                        consts.bo[:, :].unsqueeze(1).to_broadcast([P, TT, D]), ALU.add
                                        ).then_inc(a_read, 1)
                v.wait_ge(a_read, n + 1)
                ln_a.variance(Chain(v, chain_a, n * LN_MARKS), attn, var_a)

            def add_attention(b, c, n):
                v.wait_ge(std_a, n + 1)
                ln_a.normalise(Chain(v, chain_a, n * LN_MARKS + LN_MARKS - 1), attn, attn).then_inc(norm_a, 1)
                v.wait_ge(norm_a, n + 1)
                v.wait_ge(x_ld[c % 2], (b * 2 + c // 2 + 1) * 16)
                nc.vector.tensor_tensor(x1[:, c], x_sb[:, c % 2], attn[:, :, :], ALU.add).then_inc(x1_done, 1)
                v.wait_ge(x1_done, n + 1)
                ln_x.variance(Chain(v, chain_x, n * LN_MARKS), x1[:, c], var_x)

            def normalise_x1(b, c, n):
                v.wait_ge(std_x, n + 1)
                wait_for(v, y_turned, n)
                ln_x.normalise(Chain(v, chain_x, n * LN_MARKS + LN_MARKS - 1), x1[:, c], y).then_inc(y_done, 1)

            def route(b):
                chain = Chain(v, chain_r, b * 9)
                v.wait_ge(logits, b + 1)
                chain.mark(nc.vector.tensor_tensor(rt[:, 0], psA[0:1, 0, 0:E], consts.br[:, :], ALU.add))
                for i in range(2):
                    score, equal, where = rt[:, 3 * i], rt[:, 3 * i + 1], rt[:, 3 * i + 2]
                    top, at = best[:, 2 * i:2 * i + 1], best[:, 2 * i + 1:2 * i + 2]
                    chain.wait()
                    chain.mark(nc.vector.tensor_reduce(top, score, AX.X, ALU.max))
                    chain.wait()
                    chain.mark(nc.vector.scalar_tensor_tensor(out=where, in0=score, scalar=top, in1=place[:, :],
                                                              op0=ALU.is_equal, op1=ALU.mult))
                    chain.wait()
                    chain.mark(nc.vector.tensor_reduce(at, where, AX.X, ALU.min))
                    chain.wait()
                    if i == 0:
                        chain.mark(nc.vector.tensor_scalar(equal, place[:, :], at, -3.0e38, ALU.is_equal, ALU.mult))
                        chain.wait()
                        chain.mark(nc.vector.tensor_tensor(rt[:, 3], score, equal, ALU.add))
                nc.vector.tensor_scalar(chosen[:, :], best[:, :].rearrange("o (i two) -> o i two", two=2)[:, :, 1],
                                        float(E), None, ALU.add).then_inc(idx_done, 1)

            def experts_end(b, c, n):
                p = c % 2
                if c == 0:
                    v.wait_ge(w2_ld, (b + 1) * 16 * W_LOADS)
                    nc.vector.tensor_scalar(b2half[:, :], b2e[:, 0], 0.5, None, ALU.mult).then_inc(chain_b, 1)
                    v.wait_ge(chain_b, b * 2 + 1)
                    nc.vector.scalar_tensor_tensor(out=b2mean[:, :], in0=b2e[:, 1], scalar=0.5, in1=b2half[:, :],
                                                   op0=ALU.mult, op1=ALU.add).then_inc(chain_b, 1)
                    v.wait_ge(chain_b, b * 2 + 2)
                if isinstance(b, int):
                    v.wait_ge(out_done, n)
                v.wait_ge(o_done, n + 1)
                nc.vector.scalar_tensor_tensor(out=ffn[:, :, :], in0=psO[:, :, :], scalar=0.5,
                                               in1=b2mean[:, :].unsqueeze(1).to_broadcast([P, TT, D]),
                                               op0=ALU.mult, op1=ALU.add).then_inc(o_read, 1)
                v.wait_ge(o_read, n + 1 + 1)
                chain = Chain(v, chain_f, n * LN_MARKS)
                ln_f.variance(chain, ffn, var_f)
                v.wait_ge(std_f, n + 1)
                ln_f.normalise(chain, ffn, ffn).then_inc(norm_f, 1)
                v.wait_ge(norm_f, n + 1)
                v.wait_ge(stored[p], 16 + (b * 2 + c // 2) * 16)
                nc.vector.tensor_tensor(out_sb[:, p], x1[:, c], ffn[:, :, :], ALU.add).then_inc(out_done, 1)

            def step(b, c):
                first = isinstance(b, int) and b == -1
                if first and c == 1:
                    chunks.invert_sums(v, NPAIR - 1)
                for k, part in ((2, normalise_x1), (1, route), (3, add_attention), (0, experts_end),
                                (4, take_projection), (2, route)):
                    which = ahead(b, c, k)
                    if part is route:
                        if to_route(b, c) is not None and (k == 2) == first:
                            route(to_route(b, c))
                    elif which:
                        part(*which)

            v.wait_ge(consts.set, consts.BUILT)
            v.wait_ge(consts.loaded, 16 * consts.LOADS)
            v.sem_inc(o_read, 1)
            for p in range(2):
                v.sem_inc(stored[p], 16)
            steps(v, step)

        @block.scalar
        def _(act):
            def gelu(b, c, n):
                if c == 0:
                    act.wait_ge(w1_ld, (b + 1) * 16 * W_LOADS)
                for i in range(2 * KD):
                    e, m = divmod(i, KD)
                    act.wait_ge(h_done, n * 2 * KD + i + 1)
                    nc.scalar.activation(hT[:, e, m], psH[:, i % 2], ACT.Gelu, bias=b1e[:, e, m:m + 1]
                                         ).then_inc(gelu_done, 1)

            def root_x1(b, c, n):
                act.wait_ge(var_x, n + 1)
                ln_x.root(consts.eps, std_x)

            def copy_y(b, c, n):
                act.wait_ge(y_turned, n + 1)
                nc.scalar.copy(yT[:, :, c], psT[:, :, :]).then_inc(yT_done, 1)

            def root_attn(b, c, n):
                act.wait_ge(var_a, n + 1)
                ln_a.root(consts.eps, std_a)

            def root_ffn(b, c, n):
                act.wait_ge(var_f, n + 1)
                ln_f.root(consts.eps, std_f)

            def step(b, c):
                order = ((0, gelu), (3, root_attn), (3, root_x1), (0, root_ffn), (2, copy_y))
                for k, part in order:
                    which = ahead(b, c, k)
                    if which:
                        part(*which)

            act.sem_inc(gelu_done, 2)
            steps(act, step)

        @block.tensor
        def _(pe):
            def project(b, c, n):
                pe.wait_ge(cc_done, n + 1)
                wait_for(pe, a_read, n)
                if c == 3:
                    pe.wait_ge(idx_done, b + 1)
                for t in range(TT):
                    for k in range(KD):
                        ins_ = nc.tensor.matmul(psA[:, t], cc[:, c, k, t * P:(t + 1) * P], wo[:, k],
                                                start=(k == 0), stop=(k == KD - 1))
                ins_.then_inc(a_done, 1)

            def turn_y(b, c, n):
                pe.wait_ge(y_done, n + 1)
                wait_for(pe, yT_done, n)
                for k in range(KD):
                    for t in range(TT):
                        ins_ = nc.tensor.transpose(psT[:, k, t * P:(t + 1) * P], y[:, t, k * P:(k + 1) * P],
                                                   ident[:, :])
                ins_.then_inc(y_turned, 1)

            def score_experts(b, n):
                pe.wait_ge(yT_done, n + 1)
                pe.wait_ge(a_read, n + 3)
                for k in range(KD):
                    ins_ = nc.tensor.matmul(psA[0:1, 0, 0:E], yT[:, k, 0, 0:1], wr[:, k],
                                            start=(k == 0), stop=(k == KD - 1))
                ins_.then_inc(logits, 1)

            def hidden(b, c, n):
                if c == 0:
                    pe.wait_ge(w1_ld, (b + 1) * 16 * W_LOADS)
                pe.wait_ge(yT_done, n + 1)
                for i in range(2 * KD):
                    e, m = divmod(i, KD)
                    pe.wait_ge(gelu_done, n * 2 * KD + i - 1 + 2)
                    for k in range(KD):
                        ins_ = nc.tensor.matmul(psH[:, i % 2], w1e[:, e, k, m * P:(m + 1) * P], yT[:, k, c],
                                                start=(k == 0), stop=(k == KD - 1))
                    ins_.then_inc(h_done, 1)

            def outer(b, c, n):
                if c == 0:
                    pe.wait_ge(w2_ld, (b + 1) * 16 * W_LOADS)
                pe.wait_ge(o_read, n + 1)
                for t in range(TT):
                    for i in range(2 * KD):
                        e, m = divmod(i, KD)
                        if t == 0:
                            pe.wait_ge(gelu_done, n * 2 * KD + i + 1 + 2)
                        ins_ = nc.tensor.matmul(psO[:, t], hT[:, e, m, t * P:(t + 1) * P], w2e[:, e, m],
                                                start=(i == 0), stop=(i == 2 * KD - 1))
                ins_.then_inc(o_done, 1)

            def step(b, c):
                first = isinstance(b, int) and b == -1
                order = ((0, hidden), (1, score_experts), (0, outer), (2, turn_y), (4, project))
                if first:
                    order = ((4, project), (2, turn_y), (2, score_experts))
                for k, part in order:
                    which = ahead(b, c, k)
                    if part is score_experts:
                        if to_route(b, c) is not None and (k == 2) == first:
                            score_experts(to_route(b, c), to_route(b, c) * NC)
                    elif which:
                        part(*which)

            pe.wait_ge(consts.loaded, 16 * consts.LOADS)
            steps(pe, step)


def program(nc, ins, out):
    qk_scr = nc.dram_tensor("qk_parts", (2, 3, B * D, S), BF16, kind="Internal").ap()
    v_scr = nc.dram_tensor("v_ones", (B * NG, S, HG * VW), F32, kind="Internal").ap()
    o_scr = nc.dram_tensor("out_sums", (B * H, VW, S), F32, kind="Internal").ap()
    inv_scr = nc.dram_tensor("inverse_sums", (B * H, S), F32, kind="Internal").ap()
    with ExitStack() as outer:
        consts = Constants(nc, outer)
        chunks = Chunks(nc, outer, ins, o_scr, inv_scr)
        with ExitStack() as ctx:
            groups = Groups(nc, ctx, qk_scr, v_scr)
            stage_a(nc, ins, qk_scr, v_scr, consts, groups, chunks)
            stage_b(nc, consts, groups, chunks)
        stage_c(nc, ins, consts, chunks, out)




_NAMES = {"x": "L0_attn_x", "wq": "L0_attn_wq", "bq": "L0_attn_bq", "wk": "L0_attn_wk", "bk": "L0_attn_bk",
          "wv": "L0_attn_wv", "bv": "L0_attn_bv", "wo": "L0_attn_wo", "bo": "L0_attn_bo", "wr": "L0_ffn_Wr",
          "br": "L0_ffn_br", "w1": "L0_ffn_W1", "b1": "L0_ffn_b1", "w2": "L0_ffn_W2", "b2": "L0_ffn_b2"}


def kernel(**inputs):
    import numpy as _np
    import concourse.bacc as _bacc
    from concourse import mybir as _mybir
    from concourse.bass_utils import run_bass_kernel_spmd as _run

    nc = _bacc.Bacc("TRN2", target_bir_lowering=False, num_devices=1)
    arrays, aps = {}, {}
    for short, name in _NAMES.items():
        a = _np.ascontiguousarray(inputs[name])
        arrays[f"in_{name}"] = a
        aps[short] = nc.dram_tensor(f"in_{name}", a.shape, _mybir.dt.from_np(a.dtype), kind="ExternalInput").ap()
    out = nc.dram_tensor("out_0", (B, S, D), F32, kind="ExternalOutput").ap()
    program(nc, aps, out)
    r = _run(nc, [arrays], core_ids=[0])
    return r.results[0]["out_0"]
```
